# Optimizing a Trainium2 kernel written in Bass

```python
import numpy as np
import jax
import jax.numpy as jnp

def _softmax(x, axis=-1):
    return jax.nn.softmax(x, axis=axis)

def _gelu(x):
    return jax.nn.gelu(x, approximate=True)

def _silu(x):
    return jax.nn.silu(x)

def _sigmoid(x):
    return jax.nn.sigmoid(x)

def _layernorm(x, axis=-1, eps=1e-05):
    m = jnp.mean(x, axis=axis, keepdims=True)
    v = jnp.var(x, axis=axis, keepdims=True)
    return (x - m) / jnp.sqrt(v + eps)

def _scatter_add(tgt, idx, src, axis=0):
    return tgt.at[idx].add(src)

def _segment_sum(src, seg, n):
    return jax.ops.segment_sum(src, seg, n)
kernel_name = 'mk_gnn_preln_d2_gnn_r8_d44995'

def setup_inputs(seed: int=0):
    np.random.seed(seed)
    _w = jnp.asarray

    def _rec_inputs():
        import jax
        import jax.numpy as jnp
        _gk = jax.random.key(seed)
        x = -0.000202 + 1 * jax.random.normal(jax.random.fold_in(_gk, 1), (6250, 128), jnp.float32)
        _s = jax.random.randint(jax.random.fold_in(_gk, 2), (50000,), 0, 6250, jnp.int32)
        _d = jax.random.randint(jax.random.fold_in(_gk, 3), (50000,), 0, 6250, jnp.int32)
        _loop = jnp.arange(6250, dtype=jnp.int32)
        src = jnp.concatenate([_s, _d, _loop])
        dst = jnp.concatenate([_d, _s, _loop])
        _o = jnp.argsort(dst, stable=True)
        src = src[_o]
        dst = dst[_o]
        edge_attr_128 = -5.16925e-05 + 1.00005 * jax.random.normal(jax.random.fold_in(_gk, 11), (106250, 128), jnp.float32)
        return (x, src, dst, edge_attr_128)
    x, src, dst, edge_attr_128 = _rec_inputs()

    def _L0_gnn_setup():
        import jax, jax.numpy as jnp
        import numpy as np
        N, E, D, P = (6250, 100000, 128, 4)

        def phm_linear(h, phm_rule, W, bias):
            H = jnp.einsum('nij,nab->iajb', phm_rule, W).reshape(D, D)
            return h @ H + bias
        key = jax.random.key(seed)
        ks = jax.random.split(key, 5)
        x = jax.random.normal(ks[0], (N, D), jnp.float32)
        edge_index = jax.random.randint(ks[1], (2, E), 0, N, dtype=jnp.int32).astype(jnp.int64)
        edge_attr = jax.random.normal(ks[2], (E, D), jnp.float32)
        phm_rule = jax.random.normal(ks[3], (P, P, P), jnp.float32)
        W = jax.random.normal(ks[4], (P, D // P, D // P), jnp.float32) * np.float32(1.0 / np.sqrt(D))
        bias = jnp.zeros((D,), jnp.float32)
        beta = jnp.ones((), jnp.float32)
        return dict(x=x, edge_attr=edge_attr, phm_rule=phm_rule, W=W, bias=bias, beta=beta, edge_index=edge_index)
    _L0_gnn_all = _L0_gnn_setup()
    _L0_gnn_in = {k: v for k, v in _L0_gnn_all.items() if k in ('phm_rule', 'W', 'bias', 'beta')}
    del _L0_gnn_all

    def _L1_gnn_setup():
        import jax, jax.numpy as jnp
        import numpy as np
        N = 6250
        E = 100000
        IN_DIM = 128
        OUT_DIM = 128
        HEADS = 4
        HEAD_DIM = OUT_DIM // HEADS
        key = jax.random.key(seed)
        k1, k2, k3, k4 = jax.random.split(key, 4)
        x = jax.random.normal(k1, (N, IN_DIM), dtype=jnp.float32)
        W = jax.random.normal(k2, (OUT_DIM, IN_DIM), dtype=jnp.float32) / np.sqrt(IN_DIM)
        a = jax.random.normal(k3, (2 * HEAD_DIM,), dtype=jnp.float32) / np.sqrt(2 * HEAD_DIM)
        edge_index = jax.random.randint(k4, (2, E), 0, N, dtype=jnp.int32)
        return {'x': x, 'W': W, 'a': a, 'edge_index': edge_index}
    _L1_gnn_all = _L1_gnn_setup()
    _L1_gnn_in = {k: v for k, v in _L1_gnn_all.items() if k in ('W', 'a')}
    del _L1_gnn_all
    return {'x': x, 'src': src, 'dst': dst, 'edge_attr_128': edge_attr_128, 'L0_gnn_phm_rule': _L0_gnn_in['phm_rule'], 'L0_gnn_W': _L0_gnn_in['W'], 'L0_gnn_bias': _L0_gnn_in['bias'], 'L0_gnn_beta': _L0_gnn_in['beta'], 'L1_gnn_W': _L1_gnn_in['W'], 'L1_gnn_a': _L1_gnn_in['a']}

def reference(x, src, dst, edge_attr_128, L0_gnn_phm_rule, L0_gnn_W, L0_gnn_bias, L0_gnn_beta, L1_gnn_W, L1_gnn_a):
    import jax
    import jax.numpy as jnp

    def _L0_gnn_ref(x, edge_attr, phm_rule, W, bias, beta, edge_index):
        import jax, jax.numpy as jnp
        import numpy as np
        N, E, D, P = (6250, 100000, 128, 4)

        def phm_linear(h, phm_rule, W, bias):
            H = jnp.einsum('nij,nab->iajb', phm_rule, W).reshape(D, D)
            return h @ H + bias
        src, dst = (edge_index[0], edge_index[1])
        msg = x[src] + edge_attr
        s = msg * beta
        m = jax.ops.segment_max(s, dst, num_segments=N)
        e = jnp.exp(s - m[dst])
        denom = jax.ops.segment_sum(e, dst, num_segments=N)
        alpha = e / denom[dst]
        agg = jax.ops.segment_sum(msg * alpha, dst, num_segments=N)
        out = phm_linear(agg, phm_rule, W, bias)
        return out + x

    def _L1_gnn_ref(x, W, a, edge_index):
        import jax, jax.numpy as jnp
        import numpy as np
        N = 6250
        E = 100000
        IN_DIM = 128
        OUT_DIM = 128
        HEADS = 4
        HEAD_DIM = OUT_DIM // HEADS
        n = x.shape[0]
        Wx = (x @ W.T).reshape(n, HEADS, HEAD_DIM)
        src, dst = (edge_index[0], edge_index[1])
        h_src = Wx[src]
        h_dst = Wx[dst]
        e = jnp.einsum('ehd,d->eh', h_src, a[:HEAD_DIM]) + jnp.einsum('ehd,d->eh', h_dst, a[HEAD_DIM:])
        e = jax.nn.leaky_relu(e, negative_slope=0.2)
        m = jax.ops.segment_max(e, dst, num_segments=n)
        ex = jnp.exp(e - m[dst])
        denom = jax.ops.segment_sum(ex, dst, num_segments=n)
        alpha = ex / denom[dst]
        out = jax.ops.segment_sum(alpha[..., None] * h_src, dst, num_segments=n)
        return jax.nn.elu(out.reshape(n, OUT_DIM))
    edge_index = jnp.stack([src, dst])
    h = jnp.maximum(_layernorm(x, axis=-1), 0.0)
    x = x + _L0_gnn_ref(h, edge_attr_128, L0_gnn_phm_rule, L0_gnn_W, L0_gnn_bias, L0_gnn_beta, edge_index)
    h = jnp.maximum(_layernorm(x, axis=-1), 0.0)
    x = x + _L1_gnn_ref(h, L1_gnn_W, L1_gnn_a, edge_index)
    return x

_drawn_inputs = setup_inputs


def setup_inputs(seed=0):
    import zlib

    import numpy as np

    out = dict(_drawn_inputs(seed))
    spreads = {'L0_gnn_bias': (0.0, 0.305)}
    factors = {'L1_gnn_a': 8.0}
    for name, (base, spread) in spreads.items():
        noise = np.random.default_rng([zlib.crc32(name.encode()), seed]).standard_normal(out[name].shape)
        drawn = base * np.exp(spread * noise) if base else spread * noise
        out[name] = jnp.asarray(drawn.astype(out[name].dtype))
    for name, factor in factors.items():
        out[name] = (out[name] * factor).astype(out[name].dtype)
    return out
```

```python
import concourse.bass as bass
from concourse import mybir
from contextlib import ExitStack

F32 = mybir.dt.float32
BF16 = mybir.dt.bfloat16
I32 = mybir.dt.int32
ALU = mybir.AluOpType
ACT = mybir.ActivationFunctionType

P = 128


def sweep(eng, count, unroll, stages):

    def static_step(s):
        for lag, stage in stages:
            if 0 <= s - lag < count:
                stage(s - lag, (s - lag) % unroll, (s - lag) // unroll)

    turns = (count - 1) // unroll
    first = 1 + -(-max(lag for lag, _ in stages) // unroll)
    for s in range(first * unroll):
        static_step(s)
    with eng.Fori(first, turns) as i:
        for u in range(unroll):
            for lag, stage in stages:
                stage(i * unroll + (u - lag), (u - lag) % unroll, i if u >= lag else i - 1)
    for s in range(turns * unroll, count + max(lag for lag, _ in stages)):
        static_step(s)


def apart(eng):
    eng.nop(nofuse=True)


def later(item, n):
    return not isinstance(item, int) or item >= n


def gnn_kernel(nc, x_in, src_in, dst_in, ea_in, rule_in, w0_in, bias_in, beta_in, w1_in, a_in, out):
    N, D = x_in.shape
    E = src_in.shape[0]
    PH = rule_in.shape[0]
    DB = D // PH
    HD = a_in.shape[0] // 2
    H = D // HD
    GB = 4
    GE = GB * P
    RING = 4
    NG = -(-E // (GE * RING)) * RING
    NB = NG * GB
    CT = -(-NB // P)
    FULL = E // P
    NT = -(-N // P)
    LAST = N - (NT - 1) * P
    NBAT = -(-NT // GB)
    assert NT % GB == 1 and (NT // GB) % 2 == 0 and NG % RING == 0
    TW = D + 2 * H
    BIG = 2.0 ** 126
    NOWHERE = -100000
    EPS = 1e-5
    WIN = GE

    ctx = ExitStack()
    with ctx:
        def sb(name, shape, dt=F32):
            return ctx.enter_context(nc.sbuf_tensor(name, shape, dt))

        def sem(name):
            return ctx.enter_context(nc.semaphore(name))

        def sems(name, n):
            return [sem(f"{name}{i}") for i in range(n)]

        h_dram = nc.dram_tensor("h_dram", [N, D], F32, kind="Internal").ap()
        wx_dram = nc.dram_tensor("wx_dram", [N + WIN, TW], F32, kind="Internal").ap()
        flag_dram = nc.dram_tensor("flag_dram", [NB * P + P], BF16, kind="Internal").ap()
        blk_dram = nc.dram_tensor("blk_dram", [CT * P, 3], I32, kind="Internal").ap()

        ident = sb("ident", [P, P])
        iota_i = sb("iota_i", [P, P], I32)
        iota_f = sb("iota_f", [P, P])
        group_pick = sb("group_pick", [P, P])
        head_mask = sb("head_mask", [P, H])
        head_spread = sb("head_spread", [H, D])
        ones_row = sb("ones_row", [1, P])
        zero_row = sb("zero_row", [1, WIN], BF16)
        pad_rows = sb("pad_rows", [P, WIN // P, TW])
        beta = sb("beta", [P, 1])
        bias_row = sb("bias_row", [1, D])
        rule_rep = sb("rule_rep", [P, PH, PH])
        w0_rep = sb("w0_rep", [P, PH, DB])
        phm = sb("phm", [P, PH, DB])
        phm_term = sb("phm_term", [P, PH, DB])
        w1 = sb("w1", [P, D])
        w1_aug = sb("w1_aug", [P, TW])
        a_col = sb("a_col", [P, 2])
        a_heads = sb("a_heads", [P, 2 * H])

        dst_i = sb("dst_i", [P, CT, P], I32)
        prev_i = sb("prev_i", [P, CT, P], I32)
        src_i = sb("src_i", [P, CT, P], I32)
        dst_f = sb("dst_f", [P, CT, P])
        src_f = sb("src_f", [P, CT, P])
        start_f = sb("start_f", [P, CT, P])
        flag_b = sb("flag_b", [P, CT, P], BF16)
        blk_f = sb("blk_f", [P, CT, 3])
        blk_i = sb("blk_i", [P, CT, 3], I32)
        blk_row = sb("blk_row", [1, CT * P, 3], I32)
        meta = sb("meta", [P, CT * P // GB, 2 * GB], I32)

        nodes = sb("nodes", [P, NT, D])
        hn = sb("hn", [P, 2, GB, D])
        hT = sb("hT", [P, 2, GE])
        stats = sb("stats", [P, 2, GB, 6])
        mv = sb("mv", [P, 2, GB, 2])
        rstd = sb("rstd", [P, 2, GB])
        shift = sb("shift", [P, 2, GB])
        log_var = sb("log_var", [P, 2, GB])
        eps = sb("eps", [P, 1])
        inv = sb("inv", [P, GE])
        aggT = sb("aggT", [P, 2, GE])
        wx = sb("wx", [P, 2, GB, TW])
        pos = sb("pos", [P, 2, GE])
        elu_e = sb("elu_e", [P, 2, GE])
        fin = sb("fin", [P, 2, GE])

        acc = sb("acc", [P, 2, N + WIN])

        msg = sb("msg", [P, RING, GB, TW])
        meta_g = sb("meta_g", [P, RING, 2 * GB], I32)
        flags = sb("flags", [P, RING, GE + 1], BF16)
        window = sb("window", [P, RING, GB, H])
        score = sb("score", [P, 2, GE])
        run_max = sb("run_max", [P, 2, GE])
        seg_max = sb("seg_max", [P, 2, GE])
        diff = sb("diff", [P, 2, GE])
        drop = sb("drop", [P, RING])
        scale = sb("scale", [P, RING])
        carried = sb("carried", [P, 2])
        wgt = sb("wgt", [P, 2, GB, D])
        prod = sb("prod", [P, 2, GB, D])
        onehot = sb("onehot", [P, RING, GB, P])
        onehotT = sb("onehotT", [P, 2, GE])
        logit_v = sb("logit_v", [P, GB * H])
        logit = sb("logit", [P, 2, GB * H])
        logit_d = sb("logit_d", [P, 2, GB * H])

        sums = ctx.enter_context(nc.psum_tensor("sums", [P, 2, 2, WIN], F32))
        bank = [ctx.enter_context(nc.psum_tensor(f"bank{i}", [P, GE], F32)) for i in range(4)]

        const_ready = sem("const_ready")
        self_pool = sem("self_pool")
        pads_in = sem("pads_in")
        edges_in = sem("edges_in")
        weights_in = sem("weights_in")
        x_loaded = sem("x_loaded")
        node_pad = sem("node_pad")
        setup_dve = sem("setup_dve")
        picks_asked = sem("picks_asked")
        base_found = sem("base_found")
        key_rows = sem("key_rows")
        src_rows = sem("src_rows")
        table_T = sem("table_T")
        table_out = sem("table_out")
        flags_made = sem("flags_made")
        blk_made = sem("blk_made")
        tables_stored = sem("tables_stored")
        blk_loaded = sem("blk_loaded")
        w1T_psum = sem("w1T_psum")
        a_made = sem("a_made")
        aug_psum = sem("aug_psum")
        aug_ready = sem("aug_ready")
        phm_ready = sem("phm_ready")
        ln0_stats = sem("ln0_stats")
        ln0_h = sem("ln0_h")
        ln0_sum = sem("ln0_sum")
        h_stored = sems("h_stored", 2)
        self_ln = sem("self_ln")
        mid_agg = sem("mid_agg")
        mid_out = sem("mid_out")
        mid_stats = sem("mid_stats")
        mid_h = sem("mid_h")
        mid_hT_psum = sem("mid_hT_psum")
        mid_hT = sem("mid_hT")
        mid_wx_psum = sem("mid_wx_psum")
        mid_wx = sem("mid_wx")
        wx_stored = sems("wx_stored", 2)
        pads_stored = sem("pads_stored")
        acc_cleared = sem("acc_cleared")
        fin_agg = sem("fin_agg")
        fin_psum = sem("fin_psum")
        fin_neg = sem("fin_neg")
        fin_exp = sem("fin_exp")
        fin_pos = sem("fin_pos")
        fin_out = sem("fin_out")
        out_stored = sems("out_stored", 2)

        def layer_sems(k):
            return dict(
                loaded=sems(f"loaded{k}_", RING),
                flagged=sems(f"flagged{k}_", RING),
                windowed=sems(f"windowed{k}_", RING),
                gathered=sems(f"gathered{k}_", RING),
                msgT=sem(f"msgT{k}"),
                scored=sem(f"scored{k}"),
                scanned=sem(f"scanned{k}"),
                dropped=sem(f"dropped{k}"),
                shifted=sem(f"shifted{k}"),
                unturned=sem(f"unturned{k}"),
                weighed=sem(f"weighed{k}"),
                onehots=sem(f"onehots{k}"),
                onehotsT=sem(f"onehotsT{k}"),
                spread=sem(f"spread{k}"),
                targets=sem(f"targets{k}"),
                logits=sem(f"logits{k}"),
                multiplied=sem(f"multiplied{k}"),
                summed=sem(f"summed{k}"),
                merged=sem(f"merged{k}"),
                factored=sem(f"factored{k}"),
                acts=sem(f"acts{k}"),
            )

        L0, L1 = layer_sems(0), layer_sems(1)
        LDX = 5
        NE_DMA = 9
        W_DMA = 3 + 2 * PH + H

        self_res = sem("self_res")
        ln0_numbers, mid_numbers, steps0, steps1, ln0_rstd, mid_rstd, eps_set = (
            sem(n) for n in ("ln0_numbers", "mid_numbers", "steps0", "steps1", "ln0_rstd", "mid_rstd", "eps_set"))
        CLEAR = NBAT - 4

        def sweep_edges(eng, stages):
            sweep(eng, NG, RING, stages)

        block = ctx.enter_context(nc.Block())

        @block.sync
        def _(sp):
            def rows(flat, lo, n):
                return flat[lo:lo + n * P].rearrange("(c e) -> c e", e=P)

            step = (NT - 1) // (LDX - 1)
            for k in range(LDX - 1):
                sp.dma_start(nodes[:, k * step:(k + 1) * step, :],
                             x_in[k * step * P:(k + 1) * step * P, :].rearrange("(t p) d -> p t d", p=P)
                             ).then_inc(x_loaded, 16)
            sp.wait_ge(node_pad, 1)
            sp.dma_start(nodes[0:LAST, NT - 1, :], x_in[(NT - 1) * P:N, :]).then_inc(x_loaded, 16)
            sp.wait_ge(pads_in, 3)
            ct = CT - 1
            tail = FULL - ct * P
            for flat, tile in ((dst_in, dst_i), (src_in, src_i)):
                sp.dma_start(tile[:, 0:ct, :], flat[0:ct * P * P].rearrange("(t c e) -> c t e", c=P, e=P)
                             ).then_inc(edges_in, 16)
                sp.dma_start(tile[0:tail, ct, :], rows(flat, ct * P * P, tail)).then_inc(edges_in, 16)
                sp.dma_start(tile[tail:tail + 1, ct, 0:E - FULL * P],
                             flat[FULL * P:E].rearrange("(a e) -> a e", a=1)).then_inc(edges_in, 16)
            sp.dma_start(prev_i[0:1, 0, 1:P], dst_in[0:P - 1].rearrange("(a e) -> a e", a=1)).then_inc(edges_in, 16)
            sp.dma_start(prev_i[1:P, 0, :], rows(dst_in, P - 1, P - 1)).then_inc(edges_in, 16)
            sp.dma_start(prev_i[:, 1:ct, :], dst_in[P * P - 1:ct * P * P - 1].rearrange("(t c e) -> c t e", c=P, e=P)
                         ).then_inc(edges_in, 16)
            sp.dma_start(prev_i[0:tail, ct, :], rows(dst_in, ct * P * P - 1, tail)).then_inc(edges_in, 16)
            sp.dma_start(prev_i[tail:tail + 1, ct, 0:E - FULL * P + 1],
                         dst_in[FULL * P - 1:E].rearrange("(a e) -> a e", a=1)).then_inc(edges_in, 16)
            sp.dma_start(w1[:, :], w1_in).then_inc(weights_in, 16)
            sp.dma_start(bias_row[:, :], bias_in.rearrange("(a d) -> a d", a=1)).then_inc(weights_in, 16)
            sp.dma_start(beta[:, :], beta_in.rearrange("(a d) -> a d", a=1).to_broadcast([P, 1])).then_inc(weights_in, 16)
            for i in range(PH):
                part = slice(i * DB, (i + 1) * DB)
                sp.dma_start(rule_rep[part, :, :],
                             rule_in[:, i:i + 1, :].rearrange("n i j -> i n j").to_broadcast([DB, PH, PH])
                             ).then_inc(weights_in, 16)
                sp.dma_start(w0_rep[part, :, :], w0_in.rearrange("n a b -> a n b")).then_inc(weights_in, 16)
            for h in range(H):
                with nc.allow_non_contiguous_dma(reason="a vector of 32 numbers onto partitions"):
                    sp.dma_start(a_col[h * HD:(h + 1) * HD, :], a_in.rearrange("(k d) -> d k", k=2)
                                 ).then_inc(weights_in, 16)

            def store_h(b, u, use):
                sp.wait_ge(ln0_h, b + 1)
                if isinstance(b, int) and b == NBAT - 1:
                    sp.dma_start(h_dram[b * GE:N, :], hn[0:LAST, u, 0, :]).then_inc(h_stored[u], 16)
                else:
                    sp.dma_start(h_dram[bass.ds(b * GE, GE), :].rearrange("(t p) d -> p t d", p=P),
                                 hn[:, u, :, :]).then_inc(h_stored[u], 16)

            sweep(sp, NBAT, 2, [(0, store_h)])

            sp.wait_ge(flags_made, 1)
            sp.dma_start(flag_dram[0:ct * P * P].rearrange("(t c e) -> c t e", c=P, e=P), flag_b[:, 0:ct, :]
                         ).then_inc(tables_stored, 16)
            sp.dma_start(flag_dram[ct * P * P:NB * P + P].rearrange("(c e) -> c e", e=P),
                         flag_b[0:NB - ct * P + 1, ct, :]).then_inc(tables_stored, 16)
            sp.wait_ge(blk_made, 1)
            sp.dma_start(blk_dram.rearrange("(t c) k -> c t k", c=P), blk_i[:, :, :]).then_inc(tables_stored, 16)
            sp.wait_ge(tables_stored, 48)
            sp.dma_start(blk_row[:, :, :], blk_dram.rearrange("(a c) k -> a c k", a=1)).then_inc(blk_loaded, 16)

            def load_meta(g, s, k):
                sp.dma_start(meta_g[:, s, :], meta[:, bass.ds(g, 1), :].rearrange("p a k -> p (a k)")
                             ).then_inc(k["loaded"][s], 16)

            def load_flags(g, s, k):
                run = flag_dram[bass.ds(g * GE, GE + 1)].rearrange("(a e) -> a e", a=1)
                sp.dma_start(flags[:, s, :], run.to_broadcast([P, GE + 1])).then_inc(k["flagged"][s], 16)

            def load0(g, s, use):
                if later(g, RING):
                    sp.wait_ge(L0["multiplied"], g - (RING - 1))
                if isinstance(g, int) and (g + 1) * GE > E:
                    whole = (E - g * GE) // P
                    rest = E - g * GE - whole * P
                    if whole > 0:
                        sp.dma_start(msg[:, s, 0:whole, 0:D],
                                     ea_in[g * GE:g * GE + whole * P, :].rearrange("(b p) d -> p b d", p=P)
                                     ).then_inc(L0["loaded"][s], 16)
                    if rest > 0:
                        sp.dma_start(msg[0:rest, s, whole, 0:D], ea_in[E - rest:E, :]).then_inc(L0["loaded"][s], 16)
                else:
                    sp.dma_start(msg[:, s, :, 0:D],
                                 ea_in[bass.ds(g * GE, GE), :].rearrange("(b p) d -> p b d", p=P)
                                 ).then_inc(L0["loaded"][s], 16)
                load_meta(g, s, L0)
                load_flags(g, s, L0)

            sp.wait_ge(table_out, 2 * CT)
            sweep_edges(sp, [(0, load0)])

            sp.wait_ge(const_ready, 1)
            sp.dma_start(wx_dram[N:N + WIN, :].rearrange("(t p) d -> p t d", p=P), pad_rows[:, :, :]).then_inc(pads_stored, 16)

            def store_wx(b, u, use):
                sp.wait_ge(mid_wx, 2 * b + 2)
                if isinstance(b, int) and b == NBAT - 1:
                    sp.dma_start(wx_dram[b * GE:N, :], wx[0:LAST, u, 0, :]).then_inc(wx_stored[u], 16)
                else:
                    sp.dma_start(wx_dram[bass.ds(b * GE, GE), :].rearrange("(t p) d -> p t d", p=P),
                                 wx[:, u, :, :]).then_inc(wx_stored[u], 16)

            sweep(sp, NBAT, 2, [(0, store_wx)])
            for u in range(2):
                sp.wait_ge(wx_stored[u], 16 * ((NBAT + 1 - u) // 2))
            sp.wait_ge(pads_stored, 16)

            def load1(g, s, use):
                if later(g, RING):
                    sp.wait_ge(L1["multiplied"], g - (RING - 1))
                    sp.wait_ge(L1["targets"], g - (RING - 1))
                load_meta(g, s, L1)
                load_flags(g, s, L1)
                for b in range(GB):
                    first = sp.value_load(blk_row[0:1, bass.ds(g * GB + b, 1), 2], min_val=0, max_val=N + WIN - P)
                    sp.dma_start(window[:, s, b, :], wx_dram[bass.ds(first, P), D + H:TW]).then_inc(L1["windowed"][s], 16)

            sweep_edges(sp, [(0, load1)])

            def store_out(b, u, use):
                sp.wait_ge(fin_out, b + 1)
                if isinstance(b, int) and b == NBAT - 1:
                    sp.dma_start(out[b * GE:N, :], fin[0:LAST, u, 0:D]).then_inc(out_stored[u], 16)
                else:
                    sp.dma_start(out[bass.ds(b * GE, GE), :].rearrange("(t p) d -> p t d", p=P),
                                 fin[:, u, :].rearrange("p (t d) -> p t d", d=D)).then_inc(out_stored[u], 16)

            sweep(sp, NBAT, 2, [(0, store_out)])
            for u in range(2):
                sp.wait_ge(out_stored[u], 16 * ((NBAT + 1 - u) // 2))

        def loads0(g):
            if (g + 1) * GE <= E:
                return 2
            left = max(E - g * GE, 0)
            return 1 + (left >= P) + (left % P > 0)

        @block.gpsimd
        def _(pool):
            pool.memset(dst_i[:, CT - 1, :], NOWHERE).then_inc(pads_in, 1)
            pool.memset(prev_i[:, :, :], NOWHERE).then_inc(pads_in, 1)
            pool.memset(src_i[:, CT - 1, :], 0).then_inc(pads_in, 1)
            pool.memset(ident[:, :], 0.0).then_inc(self_pool, 1)
            pool.memset(group_pick[:, :], 0.0).then_inc(self_pool, 1)
            pool.memset(head_mask[:, :], 1.0).then_inc(self_pool, 1)
            pool.memset(head_spread[:, :], 1.0).then_inc(self_pool, 1)
            pool.wait_ge(self_pool, 4)
            pool.affine_select(out=ident[:, :], in_=ident[:, :], pattern=[[-1, P]], compare_op=ALU.not_equal,
                               fill=1.0, base=0, channel_multiplier=1).then_inc(self_pool, 1)
            pool.affine_select(out=group_pick[:, :].rearrange("p (g b) -> p g b", b=GB),
                               in_=group_pick[:, :].rearrange("p (g b) -> p g b", b=GB),
                               pattern=[[-GB, P // GB], [0, GB]], compare_op=ALU.not_equal,
                               fill=1.0, base=0, channel_multiplier=1).then_inc(self_pool, 1)
            pool.affine_select(out=head_mask[:, :], in_=head_mask[:, :], pattern=[[-HD, H]], compare_op=ALU.is_ge,
                               fill=0.0, base=0, channel_multiplier=1).then_inc(self_pool, 1)
            pool.affine_select(out=head_spread[:, :], in_=head_spread[:, :], pattern=[[1, D]], compare_op=ALU.is_ge,
                               fill=0.0, base=0, channel_multiplier=-HD).then_inc(self_pool, 1)
            pool.wait_ge(self_pool, 8)
            pool.affine_select(out=head_mask[:, :], in_=head_mask[:, :], pattern=[[HD, H]], compare_op=ALU.is_ge,
                               fill=0.0, base=HD - 1, channel_multiplier=-1).then_inc(self_pool, 1)
            pool.affine_select(out=head_spread[:, :], in_=head_spread[:, :], pattern=[[-1, D]], compare_op=ALU.is_ge,
                               fill=0.0, base=HD - 1, channel_multiplier=HD).then_inc(self_pool, 1)
            pool.iota(iota_i[:, :], pattern=[[1, P]], base=0, channel_multiplier=0).then_inc(self_pool, 1)
            pool.wait_ge(self_pool, 11)
            pool.tensor_copy(iota_f[:, :], iota_i[:, :]).then_inc(self_pool, 1)
            pool.memset(ones_row[:, :], 1.0).then_inc(self_pool, 1)
            pool.memset(zero_row[:, :], 0.0).then_inc(self_pool, 1)
            pool.memset(pad_rows[:, :, :], 0.0).then_inc(self_pool, 1)
            pool.memset(msg[:, :, :, :], 0.0).then_inc(self_pool, 1)
            pool.wait_ge(self_pool, 16)
            pool.memset(acc[:, :, :], 0.0).then_inc(const_ready, 1)

            def norm_shift(b, u, inverted, steps, done):
                n = 1 if isinstance(b, int) and b == NBAT - 1 else GB
                pool.wait_ge(inverted, 2 * b + 2)
                apart(pool)
                pool.tensor_tensor(shift[:, u, 0:n], mv[:, u, 0:n, 0], rstd[:, u, 0:n], ALU.mult).then_inc(steps, 1)
                pool.wait_ge(steps, b + 1)
                apart(pool)
                pool.tensor_scalar(shift[:, u, 0:n], shift[:, u, 0:n], -1.0, None, ALU.mult).then_inc(done, 1)

            def shift0(b, u, use):
                norm_shift(b, u, ln0_rstd, steps0, ln0_numbers)

            def residual(b, u, use):
                pool.wait_ge(ln0_h, b + 1)
                apart(pool)
                last = isinstance(b, int) and b == NBAT - 1
                t = GB if not last else 1
                tiles = nodes[:, bass.ds(b * GB, t), :] if not last else nodes[:, b * GB:b * GB + 1, :]
                pool.tensor_tensor(tiles, tiles, hn[:, u, 0:t, :], ALU.add).then_inc(ln0_sum, 1)

            sweep(pool, NBAT, 2, [(0, shift0), (1, residual)])
            for u in range(2):
                pool.wait_ge(h_stored[u], 16 * ((NBAT + 1 - u) // 2))

            def gather0(g, s, use):
                base = sum(loads0(q) for q in range(s, min(g, NG) if isinstance(g, int) else 0, RING))
                want = 16 * (base + loads0(g)) if isinstance(g, int) else 32 * (use + 1)
                pool.wait_ge(L0["loaded"][s], want)
                apart(pool)
                for b in range(GB):
                    pool.indirect_dma_start(msg[:, s, b, 0:D], None, h_dram,
                                            bass.IndirectOffsetOnAxis(ap=meta_g[:, s, b:b + 1], axis=0),
                                            compute_op=ALU.add).then_inc(L0["gathered"][s], 16)

            sweep_edges(pool, [(0, gather0)])

            def shift1(b, u, use):
                norm_shift(b, u, mid_rstd, steps1, mid_numbers)

            sweep(pool, NBAT, 2, [(0, shift1)])
            pool.wait_ge(mid_agg, CLEAR)
            pool.memset(acc[:, :, 0:CLEAR * GE], 0.0).then_inc(acc_cleared, 1)

            def gather1(g, s, use):
                pool.wait_ge(L1["loaded"][s], 16 * (use + 1))
                apart(pool)
                for b in range(GB):
                    pool.indirect_dma_start(msg[:, s, b, :], None, wx_dram,
                                            bass.IndirectOffsetOnAxis(ap=meta_g[:, s, b:b + 1], axis=0)
                                            ).then_inc(L1["gathered"][s], 16)

            sweep_edges(pool, [(0, gather1)])

        @block.scalar
        def _(act):
            def inverse_deviation(b, u, measured, used, steps):
                n = 1 if isinstance(b, int) and b == NBAT - 1 else GB
                act.wait_ge(measured, b + 1)
                if later(b, 2):
                    act.wait_ge(used, b - 1)
                act.activation(log_var[:, u, 0:n], mv[:, u, 0:n, 1], ACT.Ln, bias=eps[:, 0:1]).then_inc(steps, 1)
                act.wait_ge(steps, 2 * b + 1)
                act.activation(rstd[:, u, 0:n], log_var[:, u, 0:n], ACT.Exp, scale=-0.5).then_inc(steps, 1)

            def dev0(b, u, use):
                inverse_deviation(b, u, ln0_stats, ln0_h, ln0_rstd)

            def dev1(b, u, use):
                inverse_deviation(b, u, mid_stats, mid_h, mid_rstd)

            def h0(b, u, use):
                act.wait_ge(ln0_numbers, b + 1)
                if later(b, 2):
                    act.wait_ge(h_stored[u], 16 * use)
                    act.wait_ge(ln0_sum, b - 1)
                apart(act)
                last = isinstance(b, int) and b == NBAT - 1
                for t in range(1 if last else GB):
                    ins = act.activation(hn[:, u, t, :], nodes[:, bass.ds(b * GB + t, 1), :].rearrange("p a d -> p (a d)"),
                                         ACT.Relu, bias=shift[:, u, t:t + 1], scale=rstd[:, u, t:t + 1])
                ins.then_inc(ln0_h, 1)

            act.wait_ge(eps_set, 1)
            sweep(act, NBAT, 2, [(0, dev0), (1, h0)])

            def merge(g, s, use, k, cleared):
                par = s % 2
                act.wait_ge(k["summed"], g + 1)
                if isinstance(g, int) and g == 0:
                    if cleared is not None:
                        act.wait_ge(cleared, 2)
                    act.activation(acc[:, :, 0:WIN], sums[:, par, :, :], ACT.Copy).then_inc(k["merged"], 1)
                    return
                node = act.value_load(blk_row[0:1, bass.ds(g * GB, 1), 1], min_val=0, max_val=N - 1)
                act.wait_ge(k["factored"], g + 1)
                act.wait_ge(k["merged"], g)
                apart(act)
                act.activation(carried[:, :], acc[:, :, bass.ds(node, 1)].rearrange("p k a -> p (k a)"), ACT.Copy,
                               scale=scale[:, s:s + 1]).then_inc(k["acts"], 1)
                act.wait_ge(k["acts"], g)
                apart(act)
                act.activation(acc[:, 0, bass.ds(node, 1)], sums[:, par, 0, 0:1], ACT.Identity,
                               bias=carried[:, 0:1])
                act.activation(acc[:, 1, bass.ds(node, 1)], sums[:, par, 1, 0:1], ACT.Identity,
                               bias=carried[:, 1:2])
                act.activation(acc[:, :, bass.ds(node + 1, WIN - 1)], sums[:, par, :, 1:WIN], ACT.Copy
                               ).then_inc(k["merged"], 1)

            act.wait_ge(weights_in, 16 * W_DMA)
            act.wait_ge(blk_loaded, 16)
            act.wait_ge(const_ready, 1)

            def score0(g, s, use):
                act.wait_ge(L0["msgT"], g + 1)
                if later(g, 2):
                    act.wait_ge(L0["shifted"], g - 1)
                act.activation(score[:, s % 2, :], bank[s % 2][:, :], ACT.Copy, scale=beta[:, 0:1]
                               ).then_inc(L0["scored"], 1)

            def weigh0(g, s, use):
                act.wait_ge(L0["unturned"], g + 1)
                if later(g, 2):
                    act.wait_ge(L0["summed"], g - 1)
                act.activation(wgt[:, s % 2, :, :], bank[2 + s % 2][:, :].rearrange("p (b d) -> p b d", b=GB), ACT.Exp
                               ).then_inc(L0["weighed"], 1)
                act.wait_ge(L0["dropped"], g + 1)
                act.activation(scale[:, s:s + 1], drop[:, s:s + 1], ACT.Exp).then_inc(L0["factored"], 1)

            def merge0(g, s, use):
                merge(g, s, use, L0, None)

            sweep_edges(act, [(0, score0), (1, weigh0), (2, merge0)])

            def h1(b, u, use):
                act.wait_ge(mid_numbers, b + 1)
                last = isinstance(b, int) and b == NBAT - 1
                if later(b, 2):
                    act.wait_ge(mid_hT_psum, b - 1)
                apart(act)
                for t in range(1 if last else GB):
                    ins = act.activation(hn[:, u, t, :], nodes[:, bass.ds(b * GB + t, 1), :].rearrange("p a d -> p (a d)"),
                                         ACT.Relu, bias=shift[:, u, t:t + 1], scale=rstd[:, u, t:t + 1])
                ins.then_inc(mid_h, 1)

            def hT1(b, u, use):
                act.wait_ge(mid_hT_psum, b + 1)
                if later(b, 2):
                    act.wait_ge(mid_wx_psum, b - 1)
                w = P if isinstance(b, int) and b == NBAT - 1 else GE
                act.activation(hT[:, u, 0:w], bank[1][:, 0:w], ACT.Copy).then_inc(mid_hT, 1)

            def wx1(b, u, use):
                act.wait_ge(mid_wx_psum, b + 1)
                if later(b, 2):
                    act.wait_ge(wx_stored[u], 16 * use)
                last = isinstance(b, int) and b == NBAT - 1
                t = 1 if last else GB
                act.activation(wx[:, u, 0:t, 0:D], bank[2][:, 0:t * D].rearrange("p (t d) -> p t d", d=D), ACT.Copy
                               ).then_inc(mid_wx, 1)
                act.activation(wx[:, u, 0:t, D:TW], bank[3][:, 0:t * 2 * H].rearrange("p (t d) -> p t d", d=2 * H), ACT.Copy
                               ).then_inc(mid_wx, 1)

            sweep(act, NBAT, 2, [(1, dev1), (2, h1), (2, hT1), (2, wx1)])

            def weigh1(g, s, use):
                act.wait_ge(L1["shifted"], g + 1)
                if later(g, 2):
                    act.wait_ge(L1["summed"], g - 1)
                act.activation(wgt[:, s % 2, :, :].rearrange("p b (h d) -> p (b h) d", h=H),
                               logit_d[:, s % 2, :].rearrange("p (k a) -> p k a", a=1).to_broadcast([P, GB * H, HD]),
                               ACT.Exp).then_inc(L1["weighed"], 1)
                act.activation(scale[:, s:s + 1], bank[3][:, 64 + s:65 + s], ACT.Exp).then_inc(L1["factored"], 1)

            def spread1(g, s, use):
                act.wait_ge(L1["onehotsT"], g + 1)
                if later(g, 2):
                    act.wait_ge(L1["targets"], g - 1)
                act.activation(onehotT[:, s % 2, :], bank[0][:, :], ACT.Copy).then_inc(L1["spread"], 1)

            def merge1(g, s, use):
                merge(g, s, use, L1, acc_cleared)

            sweep_edges(act, [(2, weigh1), (0, spread1), (3, merge1)])

            def elu(b, u, use):
                act.wait_ge(fin_psum, b + 1)
                if later(b, 2):
                    act.wait_ge(fin_out, b - 1)
                last = isinstance(b, int) and b == NBAT - 1
                w = D if last else GE
                act.activation(elu_e[:, u, 0:w], bank[u][:, 0:w], ACT.Relu, scale=-1.0).then_inc(fin_neg, 1)
                act.wait_ge(fin_neg, b + 1)
                act.activation(elu_e[:, u, 0:w], elu_e[:, u, 0:w], ACT.Exp, scale=-1.0).then_inc(fin_exp, 1)

            sweep(act, NBAT, 2, [(0, elu)])

        @block.vector
        def _(dve):
            dve.memset(eps[:, :], EPS).then_inc(eps_set, 1)
            dve.memset(nodes[:, NT - 1, :], 0.0).then_inc(node_pad, 1)

            links = [0]

            def link(ins):
                links[0] += 1
                ins.then_inc(setup_dve, 1)
                dve.wait_ge(setup_dve, links[0])

            def moments(b, u, done, self_base):
                last = isinstance(b, int) and b == NBAT - 1
                n = 1 if last else GB
                apart(dve)
                for t in range(n):
                    ins = dve.bn_stats(stats[:, u, t, :], nodes[:, bass.ds(b * GB + t, 1), :].rearrange("p a d -> p (a d)"))
                ins.then_inc(self_ln, 1)
                dve.wait_ge(self_ln, self_base + b + 1)
                apart(dve)
                for t in range(n):
                    ins = dve.bn_aggr(mv[:, u, t, :], stats[:, u, t, :])
                ins.then_inc(done, 1)

            def norm0(b, u, use):
                if later(b, 2):
                    dve.wait_ge(ln0_h, b - 1)
                moments(b, u, ln0_stats, 0)

            dve.wait_ge(x_loaded, 16 * LDX)
            sweep(dve, NBAT, 2, [(0, norm0)])

            dve.wait_ge(edges_in, 16 * (NE_DMA + 2))
            link(dve.tensor_copy(dst_f[:, :, :], dst_i[:, :, :]))
            dve.tensor_copy(src_f[:, :, :], src_i[:, :, :]).then_inc(src_rows, 1)
            dve.wait_ge(base_found, 1)
            link(dve.tensor_tensor(start_f[:, :, 0], dst_f[:, :, 0], bank[0][:, 0:CT], ALU.subtract))
            link(dve.tensor_scalar(blk_f[:, :, 0], start_f[:, :, 0], 0.0, float(WIN - P), ALU.max, ALU.min))
            link(dve.tensor_copy(blk_f[:, :, 1], bank[0][:, 0:CT]))
            link(dve.tensor_tensor(blk_f[:, :, 2], blk_f[:, :, 0], blk_f[:, :, 1], ALU.add))
            dve.tensor_copy(blk_i[:, :, :], blk_f[:, :, :]).then_inc(blk_made, 1)
            link(dve.tensor_tensor(start_f[:, :, :], dst_i[:, :, :], prev_i[:, :, :], ALU.not_equal))
            dve.tensor_scalar(flag_b[:, :, :], start_f[:, :, :], -BIG, None, ALU.mult).then_inc(flags_made, 1)
            dve.tensor_tensor(dst_f[:, :, :], dst_f[:, :, :], blk_f[:, :, 2:3].to_broadcast([P, CT, P]), ALU.subtract
                              ).then_inc(key_rows, 1)
            dve.wait_ge(const_ready, 1)
            meta_t = meta[:, :, :].rearrange("p (t g) k -> p t g k", t=CT)
            for t in range(CT):
                dve.wait_ge(table_T, 2 * t + 1)
                dve.tensor_copy(meta_t[:, t, :, 0:GB], bank[2][:, 0:P].rearrange("p (g b) -> p g b", b=GB)
                                ).then_inc(table_out, 1)
                dve.wait_ge(table_T, 2 * t + 2)
                dve.tensor_copy(meta_t[:, t, :, GB:2 * GB].bitcast(F32), bank[3][:, 0:P].rearrange("p (g b) -> p g b", b=GB)
                                ).then_inc(table_out, 1)
            dve.wait_ge(weights_in, 16 * W_DMA)
            for n in range(PH):
                left = rule_rep[:, n, :].rearrange("p (j a) -> p j a", a=1).to_broadcast([P, PH, DB])
                right = w0_rep[:, n:n + 1, :].to_broadcast([P, PH, DB])
                link(dve.tensor_tensor((phm if n == 0 else phm_term)[:, :, :], left, right, ALU.mult))
                if n:
                    link(dve.tensor_tensor(phm[:, :, :], phm[:, :, :], phm_term[:, :, :], ALU.add))
            dve.sem_inc(phm_ready, 1)
            for j in range(2):
                ins = dve.tensor_scalar(a_heads[:, j * H:(j + 1) * H], head_mask[:, :], a_col[:, j:j + 1], None, ALU.mult)
            ins.then_inc(a_made, 1)
            dve.wait_ge(aug_psum, 1)
            dve.tensor_copy(w1_aug[:, 0:D], bank[0][:, 0:D])
            dve.tensor_copy(w1_aug[:, D:TW], bank[0][:, D:TW]).then_inc(aug_ready, 1)

            def one_hot(g, s, use, k):
                key = meta_g[:, s, GB:2 * GB].bitcast(F32)
                for b in range(GB):
                    ins = dve.tensor_scalar(onehot[:, s, b, :], iota_f[:, :], key[:, b:b + 1], None, ALU.is_equal)
                ins.then_inc(k["onehots"], 1)

            def segment_max(g, s, use, k, n, data):
                par = s % 2
                dve.wait_ge(k["flagged"][s], 16 * (use + 1))
                if isinstance(g, int) and g == 0:
                    before = -BIG
                else:
                    dve.wait_ge(k["dropped"], g)
                    before = run_max[0:n, 1 - par, GE - 1:GE]
                dve.tensor_tensor_scan(run_max[0:n, par, :], flags[0:n, s, 0:GE], data, before, ALU.add, ALU.max
                                       ).then_inc(k["scanned"], 1)
                dve.wait_ge(k["scanned"], 2 * g + 1)
                dve.tensor_tensor_scan(seg_max[0:n, par, ::-1], flags[0:n, s, GE:0:-1], run_max[0:n, par, ::-1], -BIG,
                                       ALU.add, ALU.max).then_inc(k["scanned"], 1)
                dve.wait_ge(k["scanned"], 2 * g + 2)
                if not (isinstance(g, int) and g == 0):
                    if later(g, 3):
                        dve.wait_ge(k["merged"], g - 2)
                    dve.tensor_scalar(drop[0:n, s:s + 1], run_max[0:n, 1 - par, GE - 1:GE], seg_max[0:n, par, 0:1], 0.0,
                                      ALU.subtract, ALU.min).then_inc(k["dropped"], 1)
                else:
                    dve.memset(drop[0:n, s:s + 1], 0.0).then_inc(k["dropped"], 1)

            def maxima0(g, s, use):
                par = s % 2
                dve.wait_ge(L0["scored"], g + 1)
                segment_max(g, s, use, L0, P, score[:, par, :])
                if later(g, 2):
                    dve.wait_ge(L0["unturned"], g - 1)
                dve.tensor_tensor(diff[:, par, :], score[:, par, :], seg_max[:, par, :], ALU.subtract
                                  ).then_inc(L0["shifted"], 1)

            def products(g, s, use, k):
                par = s % 2
                if later(g, 2):
                    dve.wait_ge(k["summed"], g - 1)
                dve.wait_ge(k["weighed"], g + 1)
                dve.tensor_tensor(prod[:, par, :, :], wgt[:, par, :, :], msg[:, s, :, 0:D], ALU.mult
                                  ).then_inc(k["multiplied"], 1)

            def one_hot0(g, s, use):
                one_hot(g, s, use, L0)

            def products0(g, s, use):
                products(g, s, use, L0)

            sweep_edges(dve, [(0, maxima0), (1, one_hot0), (1, products0)])

            dve.wait_ge(L0["merged"], NG)

            def average(b, u, use, k_sem, used):
                last = isinstance(b, int) and b == NBAT - 1
                w = LAST if last else GE
                cols = bass.ds(b * GE, w)
                if later(b, 1):
                    dve.wait_ge(k_sem, 2 * b)
                if later(b, 2):
                    dve.wait_ge(used, b - 1)
                dve.reciprocal(inv[:, 0:w], acc[:, 1, cols]).then_inc(k_sem, 1)
                dve.wait_ge(k_sem, 2 * b + 1)
                dve.tensor_tensor(aggT[:, u, 0:w], acc[:, 0, cols], inv[:, 0:w], ALU.mult).then_inc(k_sem, 1)

            def average0(b, u, use):
                average(b, u, use, mid_agg, mid_out)

            def finish0(b, u, use):
                last = isinstance(b, int) and b == NBAT - 1
                t = 1 if last else GB
                rows = LAST if last else P
                dve.wait_ge(mid_out, b + 1)
                tiles = nodes[0:rows, b * GB:b * GB + 1, :] if last else nodes[:, bass.ds(b * GB, GB), :]
                dve.tensor_tensor(tiles, tiles, sums[0:rows, u, 0, 0:t * D].rearrange("p (t d) -> p t d", d=D), ALU.add
                                  ).then_inc(self_res, 1)
                if later(b, 2):
                    dve.wait_ge(mid_h, b - 1)
                dve.wait_ge(self_res, b + 1)
                moments(b, u, mid_stats, NBAT)

            sweep(dve, NBAT, 2, [(1, finish0), (0, average0)])
            dve.memset(acc[:, :, CLEAR * GE:N + WIN], 0.0).then_inc(acc_cleared, 1)

            def one_hot1(g, s, use):
                if later(g, RING):
                    dve.wait_ge(L1["summed"], g - (RING - 1))
                dve.wait_ge(L1["loaded"][s], 16 * (use + 1))
                one_hot(g, s, use, L1)

            def logits1(g, s, use):
                dve.wait_ge(L1["gathered"][s], 64 * (use + 1))
                dve.wait_ge(L1["targets"], g + 1)
                dve.tensor_tensor(logit_v[:, :].rearrange("p (b h) -> p b h", h=H),
                                  bank[2][:, 0:GB * H].rearrange("p (b h) -> p b h", h=H),
                                  msg[:, s, :, D:D + H], ALU.add).then_inc(L1["logits"], 1)
                dve.wait_ge(L1["logits"], 2 * g + 1)
                dve.scalar_tensor_tensor(logit[:, s % 2, :], logit_v[:, :], 0.2, logit_v[:, :], ALU.mult, ALU.max
                                         ).then_inc(L1["logits"], 1)

            def maxima1(g, s, use):
                dve.wait_ge(L1["msgT"], g + 1)
                segment_max(g, s, use, L1, H, bank[1][0:H, :])

            def shift1(g, s, use):
                dve.wait_ge(L1["unturned"], g + 1)
                if later(g, 2):
                    dve.wait_ge(L1["weighed"], g - 1)
                dve.tensor_tensor(logit_d[:, s % 2, :], logit[:, s % 2, :], bank[3][:, 0:GB * H], ALU.subtract
                                  ).then_inc(L1["shifted"], 1)

            def products1(g, s, use):
                products(g, s, use, L1)

            sweep_edges(dve, [(2, maxima1), (0, one_hot1), (2, shift1), (1, logits1), (2, products1)])

            dve.wait_ge(L1["merged"], NG)

            def average1(b, u, use):
                average(b, u, use, fin_agg, fin_psum)

            def finish1(b, u, use):
                last = isinstance(b, int) and b == NBAT - 1
                t = 1 if last else GB
                w = t * D
                dve.wait_ge(fin_neg, b + 1)
                tiles = nodes[:, b * GB:b * GB + 1, :] if last else nodes[:, bass.ds(b * GB, GB), :]
                r = LAST if last else P
                dve.scalar_tensor_tensor(pos[0:r, u, 0:w].rearrange("p (t d) -> p t d", d=D),
                                         bank[u][0:r, 0:w].rearrange("p (t d) -> p t d", d=D), 0.0, tiles[0:r],
                                         ALU.max, ALU.add).then_inc(fin_pos, 1)
                dve.wait_ge(fin_pos, b + 1)
                dve.wait_ge(fin_exp, b + 1)
                if later(b, 2):
                    dve.wait_ge(out_stored[u], 16 * use)
                dve.scalar_tensor_tensor(fin[0:r, u, 0:w], elu_e[0:r, u, 0:w], -1.0, pos[0:r, u, 0:w], ALU.add, ALU.add
                                         ).then_inc(fin_out, 1)

            sweep(dve, NBAT, 2, [(0, average1), (1, finish1)])

        @block.tensor
        def _(pe):
            pe.wait_ge(const_ready, 1)
            pe.wait_ge(setup_dve, 1)
            pe.matmul(bank[0][:, 0:CT], group_pick[:, :], dst_f[:, :, 0], start=True, stop=True).then_inc(base_found, 1)
            pe.wait_ge(src_rows, 1)
            pe.wait_ge(key_rows, 1)
            for t in range(CT):
                if t:
                    pe.wait_ge(table_out, 2 * t - 1)
                pe.transpose(bank[2][:, 0:P], src_f[:, t, :], ident[:, :]).then_inc(table_T, 1)
                if t:
                    pe.wait_ge(table_out, 2 * t)
                pe.transpose(bank[3][:, 0:P], dst_f[:, t, :], ident[:, :]).then_inc(table_T, 1)
            pe.wait_ge(weights_in, 16 * W_DMA)
            pe.wait_ge(a_made, 1)
            pe.transpose(bank[0][:, 0:D], w1[:, :], ident[:, :])
            pe.matmul(bank[0][:, D:TW], w1[:, :], a_heads[:, :], start=True, stop=True).then_inc(aug_psum, 1)
            pe.wait_ge(aug_ready, 1)
            pe.wait_ge(blk_loaded, 16)

            def segment_sums(g, s, use, k, free):
                par = s % 2
                pe.wait_ge(k["onehots"], g + 1)
                pe.wait_ge(k["multiplied"], g + 1)
                if later(g, 2):
                    pe.wait_ge(k["merged"], g - 1)
                for j in range(2):
                    pe.matmul(sums[:, par, j, :], zero_row[0:1, 0:P], zero_row[0:1, :], start=True, stop=False,
                              skip_group_check=True)
                for b in range(GB):
                    off = 0 if b == 0 else pe.value_load(blk_row[0:1, bass.ds(g * GB + b, 1), 0], min_val=0, max_val=WIN - P)
                    for j, what in enumerate((prod, wgt)):
                        ins = pe.matmul(sums[:, par, j, bass.ds(off, P)], what[:, par, b, :], onehot[:, s, b, :],
                                        start=False, stop=(b == GB - 1), skip_group_check=True)
                ins.then_inc(k["summed"], 1)

            def turn0(g, s, use):
                pe.wait_ge(L0["gathered"][s], 64 * (use + 1))
                if later(g, 2):
                    pe.wait_ge(L0["scored"], g - 1)
                for b in range(GB):
                    ins = pe.transpose(bank[s % 2][:, b * P:(b + 1) * P], msg[:, s, b, 0:D], ident[:, :])
                ins.then_inc(L0["msgT"], 1)

            def unturn0(g, s, use):
                pe.wait_ge(L0["shifted"], g + 1)
                if later(g, 2):
                    pe.wait_ge(L0["weighed"], g - 1)
                for b in range(GB):
                    ins = pe.transpose(bank[2 + s % 2][:, b * P:(b + 1) * P], diff[:, s % 2, b * P:(b + 1) * P], ident[:, :])
                ins.then_inc(L0["unturned"], 1)

            def sums0(g, s, use):
                segment_sums(g, s, use, L0, None)

            sweep_edges(pe, [(0, turn0), (1, unturn0), (2, sums0)])

            pe.wait_ge(phm_ready, 1)

            def layer_out(b, u, use):
                last = isinstance(b, int) and b == NBAT - 1
                pe.wait_ge(mid_agg, 2 * b + 2)
                if later(b, 2):
                    pe.wait_ge(self_res, b - 1)
                elif b == 0:
                    pe.wait_ge(L0["merged"], NG)
                for t in range(1 if last else GB):
                    rows = LAST if last else P
                    where = sums[0:rows, u, 0, t * D:(t + 1) * D]
                    pe.matmul(where, aggT[:, u, t * P:t * P + rows], phm[:, :, :].rearrange("p j b -> p (j b)"),
                              start=True, stop=False, skip_group_check=True)
                    ins = pe.matmul(where, ones_row[0:1, 0:rows], bias_row[0:1, :], start=False, stop=True,
                                    skip_group_check=True)
                ins.then_inc(mid_out, 1)

            def layer_in(b, u, use):
                last = isinstance(b, int) and b == NBAT - 1
                n = 1 if last else GB
                pe.wait_ge(mid_h, b + 1)
                if later(b, 1):
                    pe.wait_ge(mid_hT, b)
                for t in range(n):
                    ins = pe.transpose(bank[1][:, t * P:(t + 1) * P], hn[:, u, t, :], ident[:, :])
                ins.then_inc(mid_hT_psum, 1)
                pe.wait_ge(mid_hT, b + 1)
                if later(b, 1):
                    pe.wait_ge(mid_wx, 2 * b)
                for t in range(n):
                    pe.matmul(bank[2][:, t * D:(t + 1) * D], hT[:, u, t * P:(t + 1) * P], w1_aug[:, 0:D],
                              start=True, stop=True)
                    ins = pe.matmul(bank[3][:, t * 2 * H:(t + 1) * 2 * H], hT[:, u, t * P:(t + 1) * P], w1_aug[:, D:TW],
                                    start=True, stop=True)
                ins.then_inc(mid_wx_psum, 1)

            sweep(pe, NBAT, 2, [(0, layer_out), (2, layer_in)])
            pe.wait_ge(mid_wx, 2 * NBAT)
            pe.wait_ge(mid_stats, NBAT)

            def onehotT1(g, s, use):
                pe.wait_ge(L1["onehots"], g + 1)
                if later(g, 1):
                    pe.wait_ge(L1["spread"], g)
                for b in range(GB):
                    ins = pe.transpose(bank[0][:, b * P:(b + 1) * P], onehot[:, s, b, :], ident[:, :])
                ins.then_inc(L1["onehotsT"], 1)

            def targets1(g, s, use):
                pe.wait_ge(L1["spread"], g + 1)
                pe.wait_ge(L1["windowed"][s], 16 * GB * (use + 1))
                if later(g, 1):
                    pe.wait_ge(L1["logits"], 2 * g - 1)
                for b in range(GB):
                    ins = pe.matmul(bank[2][:, b * H:(b + 1) * H], onehotT[:, s % 2, b * P:(b + 1) * P], window[:, s, b, :],
                                    start=True, stop=True)
                ins.then_inc(L1["targets"], 1)

            def turn1(g, s, use):
                pe.wait_ge(L1["logits"], 2 * g + 2)
                if later(g, 1):
                    pe.wait_ge(L1["scanned"], 2 * g - 1)
                for b in range(GB):
                    ins = pe.transpose(bank[1][0:H, b * P:(b + 1) * P], logit[:, s % 2, b * H:(b + 1) * H], ident[:, :])
                ins.then_inc(L1["msgT"], 1)

            def unturn1(g, s, use):
                pe.wait_ge(L1["dropped"], g + 1)
                if later(g, 1):
                    pe.wait_ge(L1["shifted"], g)
                if later(g, 1):
                    pe.wait_ge(L1["factored"], g)
                pe.matmul(bank[3][:, 64 + s:65 + s], head_spread[:, :], drop[0:H, s:s + 1], start=True, stop=True)
                for b in range(GB):
                    ins = pe.transpose(bank[3][:, b * H:(b + 1) * H], seg_max[0:H, s % 2, b * P:(b + 1) * P], ident[0:H, 0:H])
                ins.then_inc(L1["unturned"], 1)

            def sums1(g, s, use):
                segment_sums(g, s, use, L1, None)

            sweep_edges(pe, [(2, unturn1), (0, onehotT1), (1, turn1), (0, targets1), (2, sums1)])

            def turn_out(b, u, use):
                last = isinstance(b, int) and b == NBAT - 1
                pe.wait_ge(fin_agg, 2 * b + 2)
                if later(b, 2):
                    pe.wait_ge(fin_pos, b - 1)
                    pe.wait_ge(fin_neg, b - 1)
                for t in range(1 if last else GB):
                    ins = pe.transpose(bank[u][0:P, t * D:(t + 1) * D], aggT[:, u, t * P:(t + 1) * P], ident[:, :])
                ins.then_inc(fin_psum, 1)

            sweep(pe, NBAT, 2, [(0, turn_out)])


_INS = ["x", "src", "dst", "edge_attr_128", "L0_gnn_phm_rule", "L0_gnn_W", "L0_gnn_bias", "L0_gnn_beta",
        "L1_gnn_W", "L1_gnn_a"]


def kernel(**inputs):
    import numpy as _np
    import concourse.bacc as _bacc
    from concourse.bass_utils import run_bass_kernel_spmd as _run

    nc = _bacc.Bacc("TRN2", target_bir_lowering=False, num_devices=1)
    arrays, args = {}, []
    for name in _INS:
        a = _np.ascontiguousarray(inputs[name])
        if a.ndim == 0:
            a = a.reshape(1)
        arrays[f"in_{name}"] = a
        args.append(nc.dram_tensor(f"in_{name}", a.shape, mybir.dt.from_np(a.dtype), kind="ExternalInput").ap())
    shape = _np.asarray(inputs["x"]).shape
    args.append(nc.dram_tensor("out_0", shape, F32, kind="ExternalOutput").ap())
    gnn_kernel(nc, *args)
    r = _run(nc, [arrays], core_ids=[0])
    return r.results[0]["out_0"]
```

```python
import concourse.bass as bass
from concourse import mybir
from contextlib import ExitStack

F32 = mybir.dt.float32
BF16 = mybir.dt.bfloat16
I32 = mybir.dt.int32
ALU = mybir.AluOpType
ACT = mybir.ActivationFunctionType

P = 128


def sweep(eng, count, unroll, stages, reach=2):

    def static_step(s):
        for lag, stage in stages:
            if 0 <= s - lag < count:
                stage(s - lag, (s - lag) % unroll, (s - lag) // unroll)

    turns = (count - 1) // unroll
    first = -(-(max(lag for lag, _ in stages) + reach) // unroll)
    for s in range(first * unroll):
        static_step(s)
    with eng.Fori(first, turns) as i:
        for u in range(unroll):
            for lag, stage in stages:
                stage(i * unroll + (u - lag), (u - lag) % unroll, i if u >= lag else i - 1)
    for s in range(turns * unroll, count + max(lag for lag, _ in stages)):
        static_step(s)


def apart(eng):
    eng.nop(nofuse=True)


def later(item, n):
    return not isinstance(item, int) or item >= n


def gnn_kernel(nc, x_in, src_in, dst_in, ea_in, rule_in, w0_in, bias_in, beta_in, w1_in, a_in, out):
    N, D = x_in.shape
    E = src_in.shape[0]
    PH = rule_in.shape[0]
    DB = D // PH
    HD = a_in.shape[0] // 2
    H = D // HD
    GB = 4
    GE = GB * P
    RING = 8
    NG = -(-E // (GE * RING)) * RING
    NB = NG * GB
    CT = -(-NB // P)
    FULL = E // P
    NT = -(-N // P)
    LAST = N - (NT - 1) * P
    NBAT = -(-NT // GB)
    assert NT % GB == 1 and (NT // GB) % 2 == 0 and NG % RING == 0
    TW = D + 2 * H
    BIG = 2.0 ** 126
    NOWHERE = -100000
    EPS = 1e-5
    WIN = GE
    HALF = RING // 2
    OFF = 512
    WGT = 4

    ctx = ExitStack()
    with ctx:
        def sb(name, shape, dt=F32):
            return ctx.enter_context(nc.sbuf_tensor(name, shape, dt))

        def sem(name):
            return ctx.enter_context(nc.semaphore(name))

        def sems(name, n):
            return [sem(f"{name}{i}") for i in range(n)]

        h_dram = nc.dram_tensor("h_dram", [N, D], F32, kind="Internal").ap()
        wx_dram = nc.dram_tensor("wx_dram", [N + WIN, TW], F32, kind="Internal").ap()
        flag_dram = nc.dram_tensor("flag_dram", [NB * P + P], BF16, kind="Internal").ap()
        blk_dram = nc.dram_tensor("blk_dram", [2, CT * P], I32, kind="Internal").ap()

        ident = sb("ident", [P, P])
        iota_i = sb("iota_i", [P, P], I32)
        iota_f = sb("iota_f", [P, P])
        group_pick = sb("group_pick", [P, P])
        head_mask = sb("head_mask", [P, H])
        head_spread = sb("head_spread", [H, D])
        ones_row = sb("ones_row", [1, P])
        junk = sb("junk", [1, 1])
        zero_row = sb("zero_row", [1, WIN], BF16)
        beta = sb("beta", [P, 1])
        bias_row = sb("bias_row", [1, D])
        rule_rep = sb("rule_rep", [P, PH, PH])
        w0_rep = sb("w0_rep", [P, PH, DB])
        phm = sb("phm", [P, PH, DB])
        phm_term = sb("phm_term", [P, PH, DB])
        w1 = sb("w1", [P, D])
        w1_aug = sb("w1_aug", [P, TW])
        a_col = sb("a_col", [P, 2])
        a_heads = sb("a_heads", [P, 2 * H])

        flag_b = sb("flag_b", [P, CT, P], BF16)
        blk_f = sb("blk_f", [P, CT, 3])
        blk_i = sb("blk_i", [P, 2, CT], I32)
        blk_row = sb("blk_row", [1, 2, CT * P], I32)
        packed = sb("packed", [1, CT * P // GB], I32)
        part = sb("part", [1, CT * P // GB], I32)
        meta = sb("meta", [P, CT * P // GB, 2 * GB], I32)

        nodes = sb("nodes", [P, NT, D])
        hn = sb("hn", [P, 2, GB, D])
        hT = sb("hT", [P, 2, GE])
        stats = sb("stats", [P, 2, GB, 6])
        mv = sb("mv", [P, 2, GB, 2])
        rstd = sb("rstd", [P, 2, GB])
        shift = sb("shift", [P, 2, GB])
        log_var = sb("log_var", [P, 2, GB])
        eps = sb("eps", [P, 1])
        inv = sb("inv", [P, GE])
        aggT = sb("aggT", [P, 2, GE])
        wx = sb("wx", [P, 2, GB, TW])
        pos = sb("pos", [P, 2, GE])
        elu_e = sb("elu_e", [P, 2, GE])
        fin = sb("fin", [P, 2, GE])

        def over(buffer):
            flat = buffer[:, :, :] if len(buffer.shape) == 3 else buffer[:, :, :, :].rearrange("p a b c -> p a (b c)")
            return flat.rearrange("p a b -> p (a b)")[:, 0:CT * P].rearrange("p (t e) -> p t e", e=P)

        dst_i, prev_i, src_i = (over(b).bitcast(I32) for b in (pos, elu_e, fin))
        dst_f, src_f, start_f = (over(b) for b in (aggT, hT, wx))

        acc = sb("acc", [P, 2, N + WIN])

        msg = sb("msg", [P, RING, GB, TW])
        meta_g = sb("meta_g", [P, RING, 2 * GB], I32)
        flags = sb("flags", [P, 2, HALF * GE + 1], BF16)
        window = sb("window", [P, RING, GB, H])
        score = sb("score", [P, 2, GE])
        run_max = sb("run_max", [P, 2, GE])
        seg_max = sb("seg_max", [P, 2, GE])
        diff = sb("diff", [P, 2, GE])
        drop = sb("drop", [P, RING])
        scale = sb("scale", [P, RING])
        carried = sb("carried", [P, 2])
        wgt = sb("wgt", [P, WGT, GB, D])
        prod = sb("prod", [P, 2, GB, D])
        onehot = sb("onehot", [P, RING, GB, P])
        onehotT = sb("onehotT", [P, 2, GE])
        logit_v = sb("logit_v", [P, GB * H])
        logit = sb("logit", [P, WGT, GB * H])
        logit_d = sb("logit_d", [P, 2, GB * H])

        sums = ctx.enter_context(nc.psum_tensor("sums", [P, 2, 2, WIN], F32))
        bank = [ctx.enter_context(nc.psum_tensor(f"bank{i}", [P, GE], F32)) for i in range(4)]

        const_ready = sem("const_ready")
        self_pool = sem("self_pool")
        pads_in = sem("pads_in")
        edges_in = sem("edges_in")
        weights_in = sem("weights_in")
        x_loaded = sem("x_loaded")
        node_pad = sem("node_pad")
        setup_dve = sem("setup_dve")
        picks_asked = sem("picks_asked")
        base_found = sem("base_found")
        key_rows = sem("key_rows")
        src_rows = sem("src_rows")
        table_T = sem("table_T")
        table_out = sem("table_out")
        flags_made = sem("flags_made")
        blk_made = sem("blk_made")
        tables_stored = sem("tables_stored")
        blk_loaded = sem("blk_loaded")
        w1T_psum = sem("w1T_psum")
        a_made = sem("a_made")
        aug_psum = sem("aug_psum")
        aug_ready = sem("aug_ready")
        phm_ready = sem("phm_ready")
        ln0_stats = sem("ln0_stats")
        ln0_h = sem("ln0_h")
        ln0_sum = sem("ln0_sum")
        h_stored = sems("h_stored", 2)
        self_ln = sem("self_ln")
        mid_agg = sem("mid_agg")
        mid_out = sem("mid_out")
        mid_stats = sem("mid_stats")
        mid_h = sem("mid_h")
        mid_hT_psum = sem("mid_hT_psum")
        mid_hT = sem("mid_hT")
        mid_wx_psum = sem("mid_wx_psum")
        mid_wx = sem("mid_wx")
        wx_stored = sems("wx_stored", 2)
        pads_stored = sem("pads_stored")
        fin_agg = sem("fin_agg")
        fin_psum = sem("fin_psum")
        fin_neg = sem("fin_neg")
        fin_exp = sem("fin_exp")
        fin_pos = sem("fin_pos")
        fin_out = sem("fin_out")
        out_stored = sems("out_stored", 2)

        def layer_sems(k):
            return dict(
                listed=sems(f"listed{k}_", 2),
                flagged=sems(f"flagged{k}_", 2),
                loaded=sems(f"loaded{k}_", RING),
                windowed=sems(f"windowed{k}_", RING),
                gathered=sems(f"gathered{k}_", RING),
                msgT=sem(f"msgT{k}"),
                scored=sem(f"scored{k}"),
                scanned=sem(f"scanned{k}"),
                dropped=sem(f"dropped{k}"),
                shifted=sem(f"shifted{k}"),
                unturned=sem(f"unturned{k}"),
                weighed=sem(f"weighed{k}"),
                onehots=sem(f"onehots{k}"),
                onehotsT=sem(f"onehotsT{k}"),
                spread=sem(f"spread{k}"),
                targets=sem(f"targets{k}"),
                logits=sem(f"logits{k}"),
                multiplied=sem(f"multiplied{k}"),
                summed=sem(f"summed{k}"),
                merged=sem(f"merged{k}"),
                factored=sem(f"factored{k}"),
                acts=sem(f"acts{k}"),
            )

        L0, L1 = layer_sems(0), layer_sems(1)
        LDX = 5
        NE_DMA = 9
        W_DMA = 3 + 2 * PH + H

        self_res = sem("self_res")
        packed_ready = sem("packed_ready")
        ln0_numbers, mid_numbers, steps0, steps1, ln0_rstd, mid_rstd, eps_set = (
            sem(n) for n in ("ln0_numbers", "mid_numbers", "steps0", "steps1", "ln0_rstd", "mid_rstd", "eps_set"))

        def sweep_edges(eng, stages):
            sweep(eng, NG, RING, stages, reach=RING)

        block = ctx.enter_context(nc.Block())

        def offsets(eng, g):
            word = eng.value_load(packed[0:1, bass.ds(g, 1)], min_val=0, max_val=(WIN - P) * (1 + OFF + OFF * OFF))
            parts = (word % OFF, word // OFF % OFF, word // (OFF * OFF))
            return [0] + [nc.s_assert_within(eng.snap(x), 0, WIN - P, skip_runtime_bounds_check_because=
                                             "9 bits each, made by a min with WIN - P") for x in parts]

        @block.sync
        def _(sp):
            def rows(flat, lo, n):
                return flat[lo:lo + n * P].rearrange("(c e) -> c e", e=P)

            step = (NT - 1) // (LDX - 1)
            for k in range(LDX - 1):
                sp.dma_start(nodes[:, k * step:(k + 1) * step, :],
                             x_in[k * step * P:(k + 1) * step * P, :].rearrange("(t p) d -> p t d", p=P)
                             ).then_inc(x_loaded, 16)
            sp.wait_ge(node_pad, 1)
            sp.dma_start(nodes[0:LAST, NT - 1, :], x_in[(NT - 1) * P:N, :]).then_inc(x_loaded, 16)
            sp.wait_ge(pads_in, 3)
            ct = CT - 1
            tail = FULL - ct * P
            for flat, tile in ((dst_in, dst_i), (src_in, src_i)):
                sp.dma_start(tile[:, 0:ct, :], flat[0:ct * P * P].rearrange("(t c e) -> c t e", c=P, e=P)
                             ).then_inc(edges_in, 16)
                sp.dma_start(tile[0:tail, ct, :], rows(flat, ct * P * P, tail)).then_inc(edges_in, 16)
                sp.dma_start(tile[tail:tail + 1, ct, 0:E - FULL * P],
                             flat[FULL * P:E].rearrange("(a e) -> a e", a=1)).then_inc(edges_in, 16)
            sp.dma_start(prev_i[0:1, 0, 1:P], dst_in[0:P - 1].rearrange("(a e) -> a e", a=1)).then_inc(edges_in, 16)
            sp.dma_start(prev_i[1:P, 0, :], rows(dst_in, P - 1, P - 1)).then_inc(edges_in, 16)
            sp.dma_start(prev_i[:, 1:ct, :], dst_in[P * P - 1:ct * P * P - 1].rearrange("(t c e) -> c t e", c=P, e=P)
                         ).then_inc(edges_in, 16)
            sp.dma_start(prev_i[0:tail, ct, :], rows(dst_in, ct * P * P - 1, tail)).then_inc(edges_in, 16)
            sp.dma_start(prev_i[tail:tail + 1, ct, 0:E - FULL * P + 1],
                         dst_in[FULL * P - 1:E].rearrange("(a e) -> a e", a=1)).then_inc(edges_in, 16)
            sp.dma_start(w1[:, :], w1_in).then_inc(weights_in, 16)
            sp.dma_start(bias_row[:, :], bias_in.rearrange("(a d) -> a d", a=1)).then_inc(weights_in, 16)
            sp.dma_start(beta[:, :], beta_in.rearrange("(a d) -> a d", a=1).to_broadcast([P, 1])).then_inc(weights_in, 16)
            for i in range(PH):
                part = slice(i * DB, (i + 1) * DB)
                sp.dma_start(rule_rep[part, :, :],
                             rule_in[:, i:i + 1, :].rearrange("n i j -> i n j").to_broadcast([DB, PH, PH])
                             ).then_inc(weights_in, 16)
                sp.dma_start(w0_rep[part, :, :], w0_in.rearrange("n a b -> a n b")).then_inc(weights_in, 16)
            for h in range(H):
                with nc.allow_non_contiguous_dma(reason="a vector of 32 numbers onto partitions"):
                    sp.dma_start(a_col[h * HD:(h + 1) * HD, :], a_in.rearrange("(k d) -> d k", k=2)
                                 ).then_inc(weights_in, 16)

            def store_h(b, u, use):
                sp.wait_ge(ln0_h, b + 1)
                if isinstance(b, int) and b == NBAT - 1:
                    sp.dma_start(h_dram[b * GE:N, :], hn[0:LAST, u, 0, :]).then_inc(h_stored[u], 16)
                else:
                    sp.dma_start(h_dram[bass.ds(b * GE, GE), :].rearrange("(t p) d -> p t d", p=P),
                                 hn[:, u, :, :]).then_inc(h_stored[u], 16)

            sweep(sp, NBAT, 2, [(0, store_h)])

            sp.wait_ge(const_ready, 1)
            sp.dma_start(wx_dram[N:N + WIN, :].rearrange("(t p) d -> p t d", p=P), msg[:, 0, :, :]
                         ).then_inc(pads_stored, 16)

            sp.wait_ge(flags_made, 1)
            sp.dma_start(flag_dram[0:ct * P * P].rearrange("(t c e) -> c t e", c=P, e=P), flag_b[:, 0:ct, :]
                         ).then_inc(tables_stored, 16)
            sp.dma_start(flag_dram[ct * P * P:NB * P + P].rearrange("(c e) -> c e", e=P),
                         flag_b[0:NB - ct * P + 1, ct, :]).then_inc(tables_stored, 16)
            sp.wait_ge(blk_made, 1)
            with nc.allow_non_contiguous_dma(reason="two numbers per block, from partitions to a row"):
                sp.dma_start(blk_dram.rearrange("k (t c) -> c k t", c=P), blk_i[:, :, :]).then_inc(tables_stored, 16)
            sp.wait_ge(tables_stored, 48)
            sp.dma_start(blk_row[:, :, :], blk_dram.rearrange("(a k) c -> a k c", a=1)).then_inc(blk_loaded, 16)

            def load_lists(g, s, use, k):
                half = slice(s, s + HALF)
                if later(g, RING):
                    sp.wait_ge(k["onehots"], g - (RING - HALF))
                    apart(sp)
                    for q in range(s, s + HALF):
                        sp.wait_ge(k["gathered"][q], 64 * use)
                    apart(sp)
                sp.dma_start(meta_g[:, half, :], meta[:, bass.ds(g, HALF), :]).then_inc(k["listed"][s // HALF], 16)

            def load_flags(g, s, k, rows):
                if later(g, RING):
                    sp.wait_ge(k["dropped"], g - (RING - HALF))
                    apart(sp)
                run = flag_dram[bass.ds(g * GE, HALF * GE + 1)].rearrange("(a e) -> a e", a=1)
                sp.dma_start(flags[0:rows, s // HALF, :], run.to_broadcast([rows, HALF * GE + 1])
                             ).then_inc(k["flagged"][s // HALF], 16)

            def load0(g, s, use):
                if s % HALF == 0:
                    load_lists(g, s, use, L0)
                if later(g, RING):
                    sp.wait_ge(L0["multiplied"], g - (RING - 1))
                if isinstance(g, int) and (g + 1) * GE > E:
                    whole = (E - g * GE) // P
                    rest = E - g * GE - whole * P
                    if whole > 0:
                        sp.dma_start(msg[:, s, 0:whole, 0:D],
                                     ea_in[g * GE:g * GE + whole * P, :].rearrange("(b p) d -> p b d", p=P)
                                     ).then_inc(L0["loaded"][s], 16)
                    if rest > 0:
                        sp.dma_start(msg[0:rest, s, whole, 0:D], ea_in[E - rest:E, :]).then_inc(L0["loaded"][s], 16)
                else:
                    sp.dma_start(msg[:, s, :, 0:D],
                                 ea_in[bass.ds(g * GE, GE), :].rearrange("(b p) d -> p b d", p=P)
                                 ).then_inc(L0["loaded"][s], 16)

            sp.wait_ge(table_out, 2 * CT)
            def flags0(g, s, use):
                if s % HALF == 0:
                    load_flags(g, s, L0, P)

            sp.wait_ge(pads_stored, 16)
            sweep_edges(sp, [(0, load0), (1, flags0)])

            def store_wx(b, u, use):
                sp.wait_ge(mid_wx, 2 * b + 2)
                if isinstance(b, int) and b == NBAT - 1:
                    sp.dma_start(wx_dram[b * GE:N, :], wx[0:LAST, u, 0, :]).then_inc(wx_stored[u], 16)
                else:
                    sp.dma_start(wx_dram[bass.ds(b * GE, GE), :].rearrange("(t p) d -> p t d", p=P),
                                 wx[:, u, :, :]).then_inc(wx_stored[u], 16)

            sweep(sp, NBAT, 2, [(0, store_wx)])
            for u in range(2):
                sp.wait_ge(wx_stored[u], 16 * ((NBAT + 1 - u) // 2))
            sp.wait_ge(packed_ready, 1)

            def load1(g, s, use):
                if s % HALF == 0:
                    load_lists(g, s, use, L1)
                if later(g, RING):
                    sp.wait_ge(L1["targets"], g - (RING - 1))
                first = sp.value_load(blk_row[0:1, 1, bass.ds(g * GB, 1)], min_val=0, max_val=N - 1)
                offset = offsets(sp, g)
                for b in range(GB):
                    sp.dma_start(window[:, s, b, :], wx_dram[bass.ds(first + offset[b], P), D + H:TW]).then_inc(L1["windowed"][s], 16)

            def flags1(g, s, use):
                if s % HALF == 0:
                    load_flags(g, s, L1, H)

            sweep_edges(sp, [(0, load1), (2, flags1)])

            def store_out(b, u, use):
                sp.wait_ge(fin_out, b + 1)
                if isinstance(b, int) and b == NBAT - 1:
                    sp.dma_start(out[b * GE:N, :], fin[0:LAST, u, 0:D]).then_inc(out_stored[u], 16)
                else:
                    sp.dma_start(out[bass.ds(b * GE, GE), :].rearrange("(t p) d -> p t d", p=P),
                                 fin[:, u, :].rearrange("p (t d) -> p t d", d=D)).then_inc(out_stored[u], 16)

            sweep(sp, NBAT, 2, [(0, store_out)])
            for u in range(2):
                sp.wait_ge(out_stored[u], 16 * ((NBAT + 1 - u) // 2))

        def loads0(g):
            if (g + 1) * GE <= E:
                return 1
            left = max(E - g * GE, 0)
            return (left >= P) + (left % P > 0)

        @block.gpsimd
        def _(pool):
            pool.memset(dst_i[:, CT - 1, :], NOWHERE).then_inc(pads_in, 1)
            pool.memset(prev_i[:, :, :], NOWHERE).then_inc(pads_in, 1)
            pool.memset(src_i[:, CT - 1, :], 0).then_inc(pads_in, 1)
            pool.memset(ident[:, :], 0.0).then_inc(self_pool, 1)
            pool.memset(group_pick[:, :], 0.0).then_inc(self_pool, 1)
            pool.memset(head_mask[:, :], 1.0).then_inc(self_pool, 1)
            pool.memset(head_spread[:, :], 1.0).then_inc(self_pool, 1)
            pool.wait_ge(self_pool, 4)
            pool.affine_select(out=ident[:, :], in_=ident[:, :], pattern=[[-1, P]], compare_op=ALU.not_equal,
                               fill=1.0, base=0, channel_multiplier=1).then_inc(self_pool, 1)
            pool.affine_select(out=group_pick[:, :].rearrange("p (g b) -> p g b", b=GB),
                               in_=group_pick[:, :].rearrange("p (g b) -> p g b", b=GB),
                               pattern=[[-GB, P // GB], [0, GB]], compare_op=ALU.not_equal,
                               fill=1.0, base=0, channel_multiplier=1).then_inc(self_pool, 1)
            pool.affine_select(out=head_mask[:, :], in_=head_mask[:, :], pattern=[[-HD, H]], compare_op=ALU.is_ge,
                               fill=0.0, base=0, channel_multiplier=1).then_inc(self_pool, 1)
            pool.affine_select(out=head_spread[:, :], in_=head_spread[:, :], pattern=[[1, D]], compare_op=ALU.is_ge,
                               fill=0.0, base=0, channel_multiplier=-HD).then_inc(self_pool, 1)
            pool.wait_ge(self_pool, 8)
            pool.affine_select(out=head_mask[:, :], in_=head_mask[:, :], pattern=[[HD, H]], compare_op=ALU.is_ge,
                               fill=0.0, base=HD - 1, channel_multiplier=-1).then_inc(self_pool, 1)
            pool.affine_select(out=head_spread[:, :], in_=head_spread[:, :], pattern=[[-1, D]], compare_op=ALU.is_ge,
                               fill=0.0, base=HD - 1, channel_multiplier=HD).then_inc(self_pool, 1)
            pool.iota(iota_i[:, :], pattern=[[1, P]], base=0, channel_multiplier=0).then_inc(self_pool, 1)
            pool.wait_ge(self_pool, 11)
            pool.tensor_copy(iota_f[:, :], iota_i[:, :]).then_inc(self_pool, 1)
            pool.memset(ones_row[:, :], 1.0).then_inc(self_pool, 1)
            pool.memset(zero_row[:, :], 0.0).then_inc(self_pool, 1)
            pool.memset(msg[:, :, :, :], 0.0).then_inc(self_pool, 1)
            pool.wait_ge(self_pool, 15)
            pool.memset(junk[:, :], 0.0).then_inc(const_ready, 1)

            def norm_shift(b, u, inverted, steps, done):
                n = 1 if isinstance(b, int) and b == NBAT - 1 else GB
                pool.wait_ge(inverted, 2 * b + 2)
                apart(pool)
                pool.tensor_tensor(shift[:, u, 0:n], mv[:, u, 0:n, 0], rstd[:, u, 0:n], ALU.mult).then_inc(steps, 1)
                pool.wait_ge(steps, b + 1)
                apart(pool)
                pool.tensor_scalar(shift[:, u, 0:n], shift[:, u, 0:n], -1.0, None, ALU.mult).then_inc(done, 1)

            def shift0(b, u, use):
                norm_shift(b, u, ln0_rstd, steps0, ln0_numbers)

            def residual(b, u, use):
                pool.wait_ge(ln0_h, b + 1)
                apart(pool)
                last = isinstance(b, int) and b == NBAT - 1
                t = GB if not last else 1
                tiles = nodes[:, bass.ds(b * GB, t), :] if not last else nodes[:, b * GB:b * GB + 1, :]
                pool.tensor_tensor(tiles, tiles, hn[:, u, 0:t, :], ALU.add).then_inc(ln0_sum, 1)

            sweep(pool, NBAT, 2, [(0, shift0), (1, residual)])
            for u in range(2):
                pool.wait_ge(h_stored[u], 16 * ((NBAT + 1 - u) // 2))

            def gather0(g, s, use):
                base = sum(loads0(q) for q in range(s, min(g, NG) if isinstance(g, int) else 0, RING))
                want = 16 * (base + loads0(g)) if isinstance(g, int) else 16 * (use + 1)
                pool.wait_ge(L0["listed"][s // HALF], 16 * (use + 1))
                pool.wait_ge(L0["loaded"][s], want)
                apart(pool)
                for b in range(GB):
                    pool.indirect_dma_start(msg[:, s, b, 0:D], None, h_dram,
                                            bass.IndirectOffsetOnAxis(ap=meta_g[:, s, b:b + 1], axis=0),
                                            compute_op=ALU.add).then_inc(L0["gathered"][s], 16)

            sweep_edges(pool, [(0, gather0)])

            def shift1(b, u, use):
                norm_shift(b, u, mid_rstd, steps1, mid_numbers)

            sweep(pool, NBAT, 2, [(0, shift1)])
            def gather1(g, s, use):
                pool.wait_ge(L1["listed"][s // HALF], 16 * (use + 1))
                if later(g, RING):
                    pool.wait_ge(L1["multiplied"], g - (RING - 1))
                apart(pool)
                for b in range(GB):
                    pool.indirect_dma_start(msg[:, s, b, :], None, wx_dram,
                                            bass.IndirectOffsetOnAxis(ap=meta_g[:, s, b:b + 1], axis=0)
                                            ).then_inc(L1["gathered"][s], 16)

            sweep_edges(pool, [(0, gather1)])

        @block.scalar
        def _(act):
            def inverse_deviation(b, u, measured, used, steps):
                n = 1 if isinstance(b, int) and b == NBAT - 1 else GB
                act.wait_ge(measured, b + 1)
                if later(b, 2):
                    act.wait_ge(used, b - 1)
                act.activation(log_var[:, u, 0:n], mv[:, u, 0:n, 1], ACT.Ln, bias=eps[:, 0:1]).then_inc(steps, 1)
                act.wait_ge(steps, 2 * b + 1)
                act.activation(rstd[:, u, 0:n], log_var[:, u, 0:n], ACT.Exp, scale=-0.5).then_inc(steps, 1)

            def dev0(b, u, use):
                inverse_deviation(b, u, ln0_stats, ln0_h, ln0_rstd)

            def dev1(b, u, use):
                inverse_deviation(b, u, mid_stats, mid_h, mid_rstd)

            def h0(b, u, use):
                act.wait_ge(ln0_numbers, b + 1)
                if later(b, 2):
                    act.wait_ge(h_stored[u], 16 * use)
                    act.wait_ge(ln0_sum, b - 1)
                apart(act)
                last = isinstance(b, int) and b == NBAT - 1
                for t in range(1 if last else GB):
                    ins = act.activation(hn[:, u, t, :], nodes[:, bass.ds(b * GB + t, 1), :].rearrange("p a d -> p (a d)"),
                                         ACT.Relu, bias=shift[:, u, t:t + 1], scale=rstd[:, u, t:t + 1])
                ins.then_inc(ln0_h, 1)

            act.wait_ge(eps_set, 1)
            sweep(act, NBAT, 2, [(0, dev0), (1, h0)])

            def merge(g, s, use, k, read_out):
                par = s % 2
                act.wait_ge(k["summed"], g + 1)
                if isinstance(g, int) and g == 0:
                    if read_out is not None:
                        act.wait_ge(read_out, 2 * NBAT)
                    act.activation(acc[:, :, 0:WIN], sums[:, par, :, :], ACT.Copy).then_inc(k["merged"], 1)
                    return
                node = act.value_load(blk_row[0:1, 1, bass.ds(g * GB, 1)], min_val=0, max_val=N - 1)
                act.wait_ge(k["factored"], g + 1)
                act.wait_ge(k["merged"], g)
                apart(act)
                act.activation(carried[:, :], acc[:, :, bass.ds(node, 1)].rearrange("p k a -> p (k a)"), ACT.Copy,
                               scale=scale[:, s:s + 1]).then_inc(k["acts"], 1)
                act.wait_ge(k["acts"], g)
                apart(act)
                act.activation(acc[:, 0, bass.ds(node, 1)], sums[:, par, 0, 0:1], ACT.Identity,
                               bias=carried[:, 0:1])
                act.activation(acc[:, 1, bass.ds(node, 1)], sums[:, par, 1, 0:1], ACT.Identity,
                               bias=carried[:, 1:2])
                act.activation(acc[:, :, bass.ds(node + 1, WIN - 1)], sums[:, par, :, 1:WIN], ACT.Copy
                               ).then_inc(k["merged"], 1)

            act.wait_ge(weights_in, 16 * W_DMA)
            act.wait_ge(blk_loaded, 16)
            act.wait_ge(const_ready, 1)

            def score0(g, s, use):
                act.wait_ge(L0["msgT"], g + 1)
                if later(g, 2):
                    act.wait_ge(L0["shifted"], g - 1)
                act.activation(score[:, s % 2, :], bank[s % 2][:, :], ACT.Copy, scale=beta[:, 0:1]
                               ).then_inc(L0["scored"], 1)

            def weigh0(g, s, use):
                act.wait_ge(L0["unturned"], g + 1)
                if later(g, WGT):
                    act.wait_ge(L0["summed"], g - (WGT - 1))
                act.activation(wgt[:, s % WGT, :, :], bank[2 + s % 2][:, :].rearrange("p (b d) -> p b d", b=GB), ACT.Exp
                               ).then_inc(L0["weighed"], 1)
                act.wait_ge(L0["dropped"], g + 1)
                act.activation(scale[:, s:s + 1], drop[:, s:s + 1], ACT.Exp).then_inc(L0["factored"], 1)

            def merge0(g, s, use):
                merge(g, s, use, L0, None)

            sweep_edges(act, [(5, merge0), (0, score0), (2, weigh0)])

            def h1(b, u, use):
                act.wait_ge(mid_numbers, b + 1)
                last = isinstance(b, int) and b == NBAT - 1
                if later(b, 2):
                    act.wait_ge(mid_hT_psum, b - 1)
                apart(act)
                for t in range(1 if last else GB):
                    ins = act.activation(hn[:, u, t, :], nodes[:, bass.ds(b * GB + t, 1), :].rearrange("p a d -> p (a d)"),
                                         ACT.Relu, bias=shift[:, u, t:t + 1], scale=rstd[:, u, t:t + 1])
                ins.then_inc(mid_h, 1)

            def hT1(b, u, use):
                act.wait_ge(mid_hT_psum, b + 1)
                if later(b, 2):
                    act.wait_ge(mid_wx_psum, b - 1)
                w = P if isinstance(b, int) and b == NBAT - 1 else GE
                act.activation(hT[:, u, 0:w], bank[1][:, 0:w], ACT.Copy).then_inc(mid_hT, 1)

            def wx1(b, u, use):
                act.wait_ge(mid_wx_psum, b + 1)
                if later(b, 2):
                    act.wait_ge(wx_stored[u], 16 * use)
                last = isinstance(b, int) and b == NBAT - 1
                t = 1 if last else GB
                act.activation(wx[:, u, 0:t, 0:D], bank[2][:, 0:t * D].rearrange("p (t d) -> p t d", d=D), ACT.Copy
                               ).then_inc(mid_wx, 1)
                act.activation(wx[:, u, 0:t, D:TW], bank[3][:, 0:t * 2 * H].rearrange("p (t d) -> p t d", d=2 * H), ACT.Copy
                               ).then_inc(mid_wx, 1)

            sweep(act, NBAT, 2, [(1, dev1), (2, h1), (2, hT1), (2, wx1)])

            def weigh1(g, s, use):
                act.wait_ge(L1["shifted"], g + 1)
                if later(g, WGT):
                    act.wait_ge(L1["summed"], g - (WGT - 1))
                act.activation(wgt[:, s % WGT, :, :].rearrange("p b (h d) -> p (b h) d", h=H),
                               logit_d[:, s % 2, :].rearrange("p (k a) -> p k a", a=1).to_broadcast([P, GB * H, HD]),
                               ACT.Exp).then_inc(L1["weighed"], 1)
                act.activation(scale[:, s:s + 1], bank[3][:, 64 + s:65 + s], ACT.Exp).then_inc(L1["factored"], 1)

            def spread1(g, s, use):
                act.wait_ge(L1["onehotsT"], g + 1)
                if later(g, 2):
                    act.wait_ge(L1["targets"], g - 1)
                act.activation(onehotT[:, s % 2, :], bank[0][:, :], ACT.Copy).then_inc(L1["spread"], 1)

            def merge1(g, s, use):
                merge(g, s, use, L1, mid_agg)

            sweep_edges(act, [(5, weigh1), (1, spread1), (8, merge1)])

            def elu(b, u, use):
                act.wait_ge(fin_psum, b + 1)
                if later(b, 2):
                    act.wait_ge(fin_out, b - 1)
                last = isinstance(b, int) and b == NBAT - 1
                w = D if last else GE
                act.activation(elu_e[:, u, 0:w], bank[u][:, 0:w], ACT.Relu, scale=-1.0).then_inc(fin_neg, 1)
                act.wait_ge(fin_neg, b + 1)
                act.activation(elu_e[:, u, 0:w], elu_e[:, u, 0:w], ACT.Exp, scale=-1.0).then_inc(fin_exp, 1)

            sweep(act, NBAT, 2, [(0, elu)])

        @block.vector
        def _(dve):
            dve.memset(eps[:, :], EPS).then_inc(eps_set, 1)
            dve.memset(nodes[:, NT - 1, :], 0.0).then_inc(node_pad, 1)

            links = [0]

            def link(ins):
                links[0] += 1
                ins.then_inc(setup_dve, 1)
                dve.wait_ge(setup_dve, links[0])

            def moments(b, u, done, self_base):
                last = isinstance(b, int) and b == NBAT - 1
                n = 1 if last else GB
                apart(dve)
                for t in range(n):
                    ins = dve.bn_stats(stats[:, u, t, :], nodes[:, bass.ds(b * GB + t, 1), :].rearrange("p a d -> p (a d)"))
                ins.then_inc(self_ln, 1)
                dve.wait_ge(self_ln, self_base + b + 1)
                apart(dve)
                for t in range(n):
                    ins = dve.bn_aggr(mv[:, u, t, :], stats[:, u, t, :])
                ins.then_inc(done, 1)

            def norm0(b, u, use):
                if later(b, 2):
                    dve.wait_ge(ln0_h, b - 1)
                moments(b, u, ln0_stats, 0)

            dve.wait_ge(x_loaded, 16 * LDX)
            sweep(dve, NBAT, 2, [(0, norm0)])

            dve.wait_ge(edges_in, 16 * (NE_DMA + 2))
            link(dve.tensor_copy(dst_f[:, :, :], dst_i[:, :, :]))
            dve.tensor_copy(src_f[:, :, :], src_i[:, :, :]).then_inc(src_rows, 1)
            dve.wait_ge(base_found, 1)
            link(dve.tensor_tensor(start_f[:, :, 0], dst_f[:, :, 0], bank[0][:, 0:CT], ALU.subtract))
            link(dve.tensor_scalar(blk_f[:, :, 0], start_f[:, :, 0], 0.0, float(WIN - P), ALU.max, ALU.min))
            link(dve.tensor_copy(blk_f[:, :, 1], bank[0][:, 0:CT]))
            link(dve.tensor_tensor(blk_f[:, :, 2], blk_f[:, :, 0], blk_f[:, :, 1], ALU.add))
            dve.tensor_copy(blk_i[:, 0, :], blk_f[:, :, 0])
            dve.tensor_copy(blk_i[:, 1, :], blk_f[:, :, 2]).then_inc(blk_made, 1)
            link(dve.tensor_tensor(start_f[:, :, :], dst_i[:, :, :], prev_i[:, :, :], ALU.not_equal))
            dve.tensor_scalar(flag_b[:, :, :], start_f[:, :, :], -BIG, None, ALU.mult).then_inc(flags_made, 1)
            dve.tensor_tensor(dst_f[:, :, :], dst_f[:, :, :], blk_f[:, :, 2:3].to_broadcast([P, CT, P]), ALU.subtract
                              ).then_inc(key_rows, 1)
            dve.wait_ge(const_ready, 1)
            meta_t = meta[:, :, :].rearrange("p (t g) k -> p t g k", t=CT)
            for t in range(CT):
                dve.wait_ge(table_T, 2 * t + 1)
                dve.tensor_copy(meta_t[:, t, :, 0:GB], bank[2][:, 0:P].rearrange("p (g b) -> p g b", b=GB)
                                ).then_inc(table_out, 1)
                dve.wait_ge(table_T, 2 * t + 2)
                dve.tensor_copy(meta_t[:, t, :, GB:2 * GB].bitcast(F32), bank[3][:, 0:P].rearrange("p (g b) -> p g b", b=GB)
                                ).then_inc(table_out, 1)
            dve.wait_ge(blk_loaded, 16)
            off_b = blk_row[0:1, 0, :].rearrange("a (g b) -> a g b", b=GB)
            link(dve.tensor_scalar(packed[:, :], off_b[:, :, 3], 9, None, ALU.logical_shift_left))
            link(dve.tensor_tensor(packed[:, :], packed[:, :], off_b[:, :, 2], ALU.bitwise_or))
            link(dve.tensor_scalar(part[:, :], packed[:, :], 9, None, ALU.logical_shift_left))
            dve.tensor_tensor(packed[:, :], part[:, :], off_b[:, :, 1], ALU.bitwise_or).then_inc(packed_ready, 1)
            dve.wait_ge(weights_in, 16 * W_DMA)
            for n in range(PH):
                left = rule_rep[:, n, :].rearrange("p (j a) -> p j a", a=1).to_broadcast([P, PH, DB])
                right = w0_rep[:, n:n + 1, :].to_broadcast([P, PH, DB])
                link(dve.tensor_tensor((phm if n == 0 else phm_term)[:, :, :], left, right, ALU.mult))
                if n:
                    link(dve.tensor_tensor(phm[:, :, :], phm[:, :, :], phm_term[:, :, :], ALU.add))
            dve.sem_inc(phm_ready, 1)
            for j in range(2):
                ins = dve.tensor_scalar(a_heads[:, j * H:(j + 1) * H], head_mask[:, :], a_col[:, j:j + 1], None, ALU.mult)
            ins.then_inc(a_made, 1)
            dve.wait_ge(aug_psum, 1)
            dve.tensor_copy(w1_aug[:, 0:D], bank[0][:, 0:D])
            dve.tensor_copy(w1_aug[:, D:TW], bank[0][:, D:TW]).then_inc(aug_ready, 1)

            def one_hot(g, s, use, k):
                if later(g, RING):
                    dve.wait_ge(k["summed"], g - (RING - 1))
                dve.wait_ge(k["listed"][s // HALF], 16 * (use + 1))
                key = meta_g[:, s, GB:2 * GB].bitcast(F32)
                for b in range(GB):
                    ins = dve.tensor_scalar(onehot[:, s, b, :], iota_f[:, :], key[:, b:b + 1], None, ALU.is_equal)
                ins.then_inc(k["onehots"], 1)

            def segment_max(g, s, use, k, n, data):
                par = s % 2
                lo = s % HALF * GE
                flag = flags[0:n, s // HALF, lo:lo + GE + 1]
                dve.wait_ge(k["flagged"][s // HALF], 16 * (use + 1))
                if isinstance(g, int) and g == 0:
                    before = -BIG
                else:
                    dve.wait_ge(k["dropped"], g)
                    before = run_max[0:n, 1 - par, GE - 1:GE]
                dve.tensor_tensor_scan(run_max[0:n, par, :], flag[:, 0:GE], data, before, ALU.add, ALU.max
                                       ).then_inc(k["scanned"], 1)
                dve.wait_ge(k["scanned"], 2 * g + 1)
                dve.tensor_tensor_scan(seg_max[0:n, par, ::-1], flag[:, GE:0:-1], run_max[0:n, par, ::-1], -BIG,
                                       ALU.add, ALU.max).then_inc(k["scanned"], 1)
                dve.wait_ge(k["scanned"], 2 * g + 2)
                if not (isinstance(g, int) and g == 0):
                    if later(g, RING):
                        dve.wait_ge(k["factored"], g - (RING - 1))
                    dve.scalar_tensor_tensor(drop[0:n, s:s + 1], run_max[0:n, 1 - par, GE - 1:GE], seg_max[0:n, par, 0:1],
                                             flag[:, 0:1], ALU.subtract, ALU.add).then_inc(k["dropped"], 1)
                else:
                    dve.memset(drop[0:n, s:s + 1], 0.0).then_inc(k["dropped"], 1)

            def maxima0(g, s, use):
                par = s % 2
                dve.wait_ge(L0["scored"], g + 1)
                segment_max(g, s, use, L0, P, score[:, par, :])
                if later(g, 2):
                    dve.wait_ge(L0["unturned"], g - 1)
                dve.tensor_tensor(diff[:, par, :], score[:, par, :], seg_max[:, par, :], ALU.subtract
                                  ).then_inc(L0["shifted"], 1)

            def products(g, s, use, k):
                par = s % 2
                if later(g, 2):
                    dve.wait_ge(k["summed"], g - 1)
                dve.wait_ge(k["weighed"], g + 1)
                dve.tensor_tensor(prod[:, par, :, :], wgt[:, s % WGT, :, :], msg[:, s, :, 0:D], ALU.mult
                                  ).then_inc(k["multiplied"], 1)


            def products0(g, s, use):
                products(g, s, use, L0)

            def one_hot0(g, s, use):
                one_hot(g, s, use, L0)

            sweep_edges(dve, [(0, one_hot0), (1, maxima0), (3, products0)])

            dve.wait_ge(L0["merged"], NG)

            def average(b, u, use, k_sem, used):
                last = isinstance(b, int) and b == NBAT - 1
                w = LAST if last else GE
                cols = bass.ds(b * GE, w)
                if later(b, 1):
                    dve.wait_ge(k_sem, 2 * b)
                if later(b, 2):
                    dve.wait_ge(used, b - 1)
                dve.reciprocal(inv[:, 0:w], acc[:, 1, cols]).then_inc(k_sem, 1)
                dve.wait_ge(k_sem, 2 * b + 1)
                dve.tensor_tensor(aggT[:, u, 0:w], acc[:, 0, cols], inv[:, 0:w], ALU.mult).then_inc(k_sem, 1)

            def average0(b, u, use):
                average(b, u, use, mid_agg, mid_out)

            def finish0(b, u, use):
                last = isinstance(b, int) and b == NBAT - 1
                t = 1 if last else GB
                rows = LAST if last else P
                dve.wait_ge(mid_out, b + 1)
                tiles = nodes[0:rows, b * GB:b * GB + 1, :] if last else nodes[:, bass.ds(b * GB, GB), :]
                dve.tensor_tensor(tiles, tiles, sums[0:rows, u, 0, 0:t * D].rearrange("p (t d) -> p t d", d=D), ALU.add
                                  ).then_inc(self_res, 1)
                if later(b, 2):
                    dve.wait_ge(mid_h, b - 1)
                dve.wait_ge(self_res, b + 1)
                moments(b, u, mid_stats, NBAT)

            sweep(dve, NBAT, 2, [(1, finish0), (0, average0)])

            def one_hot1(g, s, use):
                one_hot(g, s, use, L1)

            def logits1(g, s, use):
                dve.wait_ge(L1["gathered"][s], 64 * (use + 1))
                dve.wait_ge(L1["targets"], g + 1)
                if later(g, 1):
                    dve.wait_ge(L1["logits"], 2 * g)
                dve.tensor_tensor(logit_v[:, :].rearrange("p (b h) -> p b h", h=H),
                                  bank[2][:, 0:GB * H].rearrange("p (b h) -> p b h", h=H),
                                  msg[:, s, :, D:D + H], ALU.add).then_inc(L1["logits"], 1)
                dve.wait_ge(L1["logits"], 2 * g + 1)
                dve.scalar_tensor_tensor(logit[:, s % WGT, :], logit_v[:, :], 0.2, logit_v[:, :], ALU.mult, ALU.max
                                         ).then_inc(L1["logits"], 1)

            def maxima1(g, s, use):
                dve.wait_ge(L1["msgT"], g + 1)
                segment_max(g, s, use, L1, H, bank[1][0:H, :])

            def shift1(g, s, use):
                dve.wait_ge(L1["unturned"], g + 1)
                if later(g, 2):
                    dve.wait_ge(L1["weighed"], g - 1)
                dve.tensor_tensor(logit_d[:, s % 2, :], logit[:, s % WGT, :], bank[3][:, 0:GB * H], ALU.subtract
                                  ).then_inc(L1["shifted"], 1)

            def products1(g, s, use):
                products(g, s, use, L1)

            sweep_edges(dve, [(3, logits1), (5, shift1), (4, maxima1), (0, one_hot1), (6, products1)])

            dve.wait_ge(L1["merged"], NG)

            def average1(b, u, use):
                average(b, u, use, fin_agg, fin_psum)

            def finish1(b, u, use):
                last = isinstance(b, int) and b == NBAT - 1
                t = 1 if last else GB
                w = t * D
                dve.wait_ge(fin_neg, b + 1)
                tiles = nodes[:, b * GB:b * GB + 1, :] if last else nodes[:, bass.ds(b * GB, GB), :]
                r = LAST if last else P
                dve.scalar_tensor_tensor(pos[0:r, u, 0:w].rearrange("p (t d) -> p t d", d=D),
                                         bank[u][0:r, 0:w].rearrange("p (t d) -> p t d", d=D), 0.0, tiles[0:r],
                                         ALU.max, ALU.add).then_inc(fin_pos, 1)
                dve.wait_ge(fin_pos, b + 1)
                dve.wait_ge(fin_exp, b + 1)
                if later(b, 2):
                    dve.wait_ge(out_stored[u], 16 * use)
                dve.scalar_tensor_tensor(fin[0:r, u, 0:w], elu_e[0:r, u, 0:w], -1.0, pos[0:r, u, 0:w], ALU.add, ALU.add
                                         ).then_inc(fin_out, 1)

            sweep(dve, NBAT, 2, [(0, average1), (1, finish1)])

        @block.tensor
        def _(pe):
            pe.wait_ge(const_ready, 1)
            pe.wait_ge(setup_dve, 1)
            pe.matmul(bank[0][:, 0:CT], group_pick[:, :], dst_f[:, :, 0], start=True, stop=True).then_inc(base_found, 1)
            pe.wait_ge(src_rows, 1)
            pe.wait_ge(key_rows, 1)
            for t in range(CT):
                if t:
                    pe.wait_ge(table_out, 2 * t - 1)
                pe.transpose(bank[2][:, 0:P], src_f[:, t, :], ident[:, :]).then_inc(table_T, 1)
                if t:
                    pe.wait_ge(table_out, 2 * t)
                pe.transpose(bank[3][:, 0:P], dst_f[:, t, :], ident[:, :]).then_inc(table_T, 1)
            pe.wait_ge(weights_in, 16 * W_DMA)
            pe.wait_ge(a_made, 1)
            pe.transpose(bank[0][:, 0:D], w1[:, :], ident[:, :])
            pe.matmul(bank[0][:, D:TW], w1[:, :], a_heads[:, :], start=True, stop=True).then_inc(aug_psum, 1)
            pe.wait_ge(aug_ready, 1)
            pe.wait_ge(packed_ready, 1)

            for par in range(2):
                for j in range(2):
                    ins = pe.matmul(sums[:, par, j, :], zero_row[0:1, 0:P], zero_row[0:1, :], start=True, stop=True)

            def segment_sums(g, s, use, k, free):
                par = s % 2
                pe.wait_ge(k["onehots"], g + 1)
                pe.wait_ge(k["multiplied"], g + 1)
                if later(g, 2):
                    pe.wait_ge(k["merged"], g - 1)
                offset = offsets(pe, g)
                for b in range(GB):
                    off = offset[b]
                    for j, (what, slot) in enumerate(((prod, par), (wgt, s % WGT))):
                        ins = pe.matmul(sums[:, par, j, bass.ds(off, P)], what[:, slot, b, :], onehot[:, s, b, :],
                                        start=(b == 0), stop=(b == GB - 1), skip_group_check=True)
                ins.then_inc(k["summed"], 1)

            def turn0(g, s, use):
                pe.wait_ge(L0["gathered"][s], 64 * (use + 1))
                if later(g, 2):
                    pe.wait_ge(L0["scored"], g - 1)
                for b in range(GB):
                    ins = pe.transpose(bank[s % 2][:, b * P:(b + 1) * P], msg[:, s, b, 0:D], ident[:, :])
                ins.then_inc(L0["msgT"], 1)

            def unturn0(g, s, use):
                pe.wait_ge(L0["shifted"], g + 1)
                if later(g, 2):
                    pe.wait_ge(L0["weighed"], g - 1)
                for b in range(GB):
                    ins = pe.transpose(bank[2 + s % 2][:, b * P:(b + 1) * P], diff[:, s % 2, b * P:(b + 1) * P], ident[:, :])
                ins.then_inc(L0["unturned"], 1)

            def sums0(g, s, use):
                segment_sums(g, s, use, L0, None)

            sweep_edges(pe, [(4, sums0), (0, turn0), (2, unturn0)])

            pe.wait_ge(phm_ready, 1)

            def layer_out(b, u, use):
                last = isinstance(b, int) and b == NBAT - 1
                pe.wait_ge(mid_agg, 2 * b + 2)
                if later(b, 2):
                    pe.wait_ge(self_res, b - 1)
                elif b == 0:
                    pe.wait_ge(L0["merged"], NG)
                for t in range(1 if last else GB):
                    rows = LAST if last else P
                    where = sums[0:rows, u, 0, t * D:(t + 1) * D]
                    pe.matmul(where, aggT[:, u, t * P:t * P + rows], phm[:, :, :].rearrange("p j b -> p (j b)"),
                              start=True, stop=False, skip_group_check=True)
                    ins = pe.matmul(where, ones_row[0:1, 0:rows], bias_row[0:1, :], start=False, stop=True,
                                    skip_group_check=True)
                ins.then_inc(mid_out, 1)

            def layer_in(b, u, use):
                last = isinstance(b, int) and b == NBAT - 1
                n = 1 if last else GB
                pe.wait_ge(mid_h, b + 1)
                if later(b, 1):
                    pe.wait_ge(mid_hT, b)
                for t in range(n):
                    ins = pe.transpose(bank[1][:, t * P:(t + 1) * P], hn[:, u, t, :], ident[:, :])
                ins.then_inc(mid_hT_psum, 1)
                pe.wait_ge(mid_hT, b + 1)
                if later(b, 1):
                    pe.wait_ge(mid_wx, 2 * b)
                for t in range(n):
                    pe.matmul(bank[2][:, t * D:(t + 1) * D], hT[:, u, t * P:(t + 1) * P], w1_aug[:, 0:D],
                              start=True, stop=True)
                    ins = pe.matmul(bank[3][:, t * 2 * H:(t + 1) * 2 * H], hT[:, u, t * P:(t + 1) * P], w1_aug[:, D:TW],
                                    start=True, stop=True)
                ins.then_inc(mid_wx_psum, 1)

            sweep(pe, NBAT, 2, [(0, layer_out), (2, layer_in)])
            pe.wait_ge(mid_wx, 2 * NBAT)
            pe.wait_ge(mid_stats, NBAT)

            def onehotT1(g, s, use):
                pe.wait_ge(L1["onehots"], g + 1)
                if later(g, 1):
                    pe.wait_ge(L1["spread"], g)
                for b in range(GB):
                    ins = pe.transpose(bank[0][:, b * P:(b + 1) * P], onehot[:, s, b, :], ident[:, :])
                ins.then_inc(L1["onehotsT"], 1)

            def targets1(g, s, use):
                pe.wait_ge(L1["spread"], g + 1)
                pe.wait_ge(L1["windowed"][s], 16 * GB * (use + 1))
                if later(g, 1):
                    pe.wait_ge(L1["logits"], 2 * g - 1)
                for b in range(GB):
                    ins = pe.matmul(bank[2][:, b * H:(b + 1) * H], onehotT[:, s % 2, b * P:(b + 1) * P], window[:, s, b, :],
                                    start=True, stop=True)
                ins.then_inc(L1["targets"], 1)

            def turn1(g, s, use):
                pe.wait_ge(L1["logits"], 2 * g + 2)
                if later(g, 1):
                    pe.wait_ge(L1["scanned"], 2 * g - 1)
                for b in range(GB):
                    ins = pe.transpose(bank[1][0:H, b * P:(b + 1) * P], logit[:, s % WGT, b * H:(b + 1) * H], ident[:, :])
                ins.then_inc(L1["msgT"], 1)

            def unturn1(g, s, use):
                pe.wait_ge(L1["dropped"], g + 1)
                if later(g, 1):
                    pe.wait_ge(L1["shifted"], g)
                if later(g, 1):
                    pe.wait_ge(L1["factored"], g)
                pe.matmul(bank[3][:, 64 + s:65 + s], head_spread[:, :], drop[0:H, s:s + 1], start=True, stop=True)
                for b in range(GB):
                    ins = pe.transpose(bank[3][:, b * H:(b + 1) * H], seg_max[0:H, s % 2, b * P:(b + 1) * P], ident[0:H, 0:H])
                ins.then_inc(L1["unturned"], 1)

            def sums1(g, s, use):
                segment_sums(g, s, use, L1, None)

            sweep_edges(pe, [(4, turn1), (1, onehotT1), (7, sums1), (2, targets1), (4, unturn1)])

            def turn_out(b, u, use):
                last = isinstance(b, int) and b == NBAT - 1
                pe.wait_ge(fin_agg, 2 * b + 2)
                if later(b, 2):
                    pe.wait_ge(fin_pos, b - 1)
                    pe.wait_ge(fin_neg, b - 1)
                for t in range(1 if last else GB):
                    ins = pe.transpose(bank[u][0:P, t * D:(t + 1) * D], aggT[:, u, t * P:(t + 1) * P], ident[:, :])
                ins.then_inc(fin_psum, 1)

            sweep(pe, NBAT, 2, [(0, turn_out)])


_INS = ["x", "src", "dst", "edge_attr_128", "L0_gnn_phm_rule", "L0_gnn_W", "L0_gnn_bias", "L0_gnn_beta",
        "L1_gnn_W", "L1_gnn_a"]


def kernel(**inputs):
    import numpy as _np
    import concourse.bacc as _bacc
    from concourse.bass_utils import run_bass_kernel_spmd as _run

    nc = _bacc.Bacc("TRN2", target_bir_lowering=False, num_devices=1)
    arrays, args = {}, []
    for name in _INS:
        a = _np.ascontiguousarray(inputs[name])
        if a.ndim == 0:
            a = a.reshape(1)
        arrays[f"in_{name}"] = a
        args.append(nc.dram_tensor(f"in_{name}", a.shape, mybir.dt.from_np(a.dtype), kind="ExternalInput").ap())
    shape = _np.asarray(inputs["x"]).shape
    args.append(nc.dram_tensor("out_0", shape, F32, kind="ExternalOutput").ap())
    gnn_kernel(nc, *args)
    r = _run(nc, [arrays], core_ids=[0])
    return r.results[0]["out_0"]
```

```python
import concourse.bass as bass
from concourse import mybir
from contextlib import ExitStack

F32 = mybir.dt.float32
BF16 = mybir.dt.bfloat16
I32 = mybir.dt.int32
ALU = mybir.AluOpType
ACT = mybir.ActivationFunctionType

P = 128


def sweep(eng, count, unroll, stages, reach=2):

    def static_step(s):
        for lag, stage in stages:
            if 0 <= s - lag < count:
                stage(s - lag, (s - lag) % unroll, (s - lag) // unroll)

    turns = (count - 1) // unroll
    first = -(-(max(lag for lag, _ in stages) + reach) // unroll)
    for s in range(first * unroll):
        static_step(s)
    with eng.Fori(first, turns) as i:
        for u in range(unroll):
            for lag, stage in stages:
                stage(i * unroll + (u - lag), (u - lag) % unroll, i if u >= lag else i - 1)
    for s in range(turns * unroll, count + max(lag for lag, _ in stages)):
        static_step(s)


def apart(eng):
    eng.nop(nofuse=True)


def later(item, n):
    return not isinstance(item, int) or item >= n


def gnn_kernel(nc, x_in, src_in, dst_in, ea_in, rule_in, w0_in, bias_in, beta_in, w1_in, a_in, out):
    N, D = x_in.shape
    E = src_in.shape[0]
    PH = rule_in.shape[0]
    DB = D // PH
    HD = a_in.shape[0] // 2
    H = D // HD
    GB = 4
    GE = GB * P
    RING = 8
    NG = -(-E // (GE * RING)) * RING
    NB = NG * GB
    CT = -(-NB // P)
    FULL = E // P
    NT = -(-N // P)
    LAST = N - (NT - 1) * P
    NBAT = -(-NT // GB)
    TW = D + 2 * H
    IN_BANK = 3
    BIG = 2.0 ** 126
    NOWHERE = -100000
    EPS = 1e-5
    WIN = GE
    HALF = RING // 2
    OFF = 512
    WXB = 4
    DVE_SLOTS = (1, 3)
    WGT = 4
    assert NT % GB == 1 and (NBAT - 1) % WXB == 0 and WGT == WXB and NG % RING == 0

    ctx = ExitStack()
    with ctx:
        def sb(name, shape, dt=F32):
            return ctx.enter_context(nc.sbuf_tensor(name, shape, dt))

        def sem(name):
            return ctx.enter_context(nc.semaphore(name))

        def sems(name, n):
            return [sem(f"{name}{i}") for i in range(n)]

        h_dram = nc.dram_tensor("h_dram", [N, D], F32, kind="Internal").ap()
        wx_dram = nc.dram_tensor("wx_dram", [N + WIN, TW], F32, kind="Internal").ap()
        flag_dram = nc.dram_tensor("flag_dram", [NB * P + P], BF16, kind="Internal").ap()
        blk_dram = nc.dram_tensor("blk_dram", [2, CT * P], I32, kind="Internal").ap()

        ident = sb("ident", [P, P])
        iota_i = sb("iota_i", [P, P], I32)
        iota_f = sb("iota_f", [P, P])
        group_pick = sb("group_pick", [P, P])
        head_mask = sb("head_mask", [P, H])
        head_spread = sb("head_spread", [H, D])
        head_pick = sb("head_pick", [P, H])
        ones_row = sb("ones_row", [1, P])
        junk = sb("junk", [1, 1])
        zero_row = sb("zero_row", [1, WIN], BF16)
        beta = sb("beta", [P, 1])
        bias_row = sb("bias_row", [1, D])
        rule_rep = sb("rule_rep", [P, PH, PH])
        w0_rep = sb("w0_rep", [P, PH, DB])
        phm = sb("phm", [P, PH, DB])
        phm_term = sb("phm_term", [P, PH, DB])
        w1 = sb("w1", [P, D])
        w1_aug = sb("w1_aug", [P, TW])
        a_col = sb("a_col", [P, 2])
        a_heads = sb("a_heads", [P, 2 * H])

        flag_b = sb("flag_b", [P, CT, P], BF16)
        blk_f = sb("blk_f", [P, CT, 3])
        blk_i = sb("blk_i", [P, 2, CT], I32)
        blk_row = sb("blk_row", [1, 2, CT * P], I32)
        packed = sb("packed", [1, CT * P // GB], I32)
        part = sb("part", [1, CT * P // GB], I32)
        meta = sb("meta", [P, CT * P // GB, 2 * GB], I32)

        nodes = sb("nodes", [P, NT, D])
        hn = sb("hn", [P, 2, GB, D])
        hn_row = hn[:, :, :, :].rearrange("p u t d -> p u (t d)")
        hT = sb("hT", [P, 2, GE])
        stats = sb("stats", [P, NT, 6])
        mean_2 = sb("mean_2", [P, NT])
        spread_v = sb("spread_v", [P, NT])
        newton = sb("newton", [P, NT])
        norm = sb("norm", [P, 2, NT])
        norm_b = sb("norm_b", [P, WXB, 2, GB])
        inv = sb("inv", [P, 2, GE])
        inv_head = sb("inv_head", [P, GB * H])
        aggT = sb("aggT", [P, 2, GE])
        pos = sb("pos", [P, 2, GE])
        elu_e = sb("elu_e", [P, 2, GE])
        fin = sb("fin", [P, 2, GE])

        def over(buffer):
            flat = buffer[:, :, :] if len(buffer.shape) == 3 else buffer[:, :, :, :].rearrange("p a b c -> p a (b c)")
            return flat.rearrange("p a b -> p (a b)")[:, 0:CT * P].rearrange("p (t e) -> p t e", e=P)

        acc = sb("acc", [P, 2, N + WIN])

        msg = sb("msg", [P, RING, GB, TW])
        meta_g = sb("meta_g", [P, RING, 2 * GB], I32)
        flags = sb("flags", [P, 2, HALF * GE + 1], BF16)
        window = sb("window", [P, RING, GB, H])
        score = sb("score", [P, 2, GE])
        run_max = sb("run_max", [P, 2, GE])
        seg_max = sb("seg_max", [P, 2, GE])
        diff = sb("diff", [P, 2, GE])
        drop = sb("drop", [P, RING])
        scale = sb("scale", [P, RING])
        carried = sb("carried", [P, 2])
        wgt = sb("wgt", [P, WGT, GB, D])
        prod = sb("prod", [P, 2, GB, D])
        onehot = sb("onehot", [P, RING, GB, P])
        onehotT = sb("onehotT", [P, 2, GE])
        logit_v = sb("logit_v", [P, GB * H])
        logit = sb("logit", [P, WGT, GB * H])
        logit_d = sb("logit_d", [P, 2, GB * H])

        dst_i, prev_i, src_i = (over(b).bitcast(I32) for b in (pos, elu_e, fin))
        dst_f, src_f, start_f = (over(b) for b in (aggT, hT, seg_max))

        sums = ctx.enter_context(nc.psum_tensor("sums", [P, 2, 2, WIN], F32))
        bank = [ctx.enter_context(nc.psum_tensor(f"bank{i}", [P, GE], F32)) for i in range(4)]

        LDX = 5

        const_ready = sem("const_ready")
        self_pool = sem("self_pool")
        pads_in = sem("pads_in")
        edges_in = sem("edges_in")
        weights_in = sem("weights_in")
        x_loaded = sems("x_loaded", LDX)
        node_pad = sem("node_pad")
        setup_dve = sem("setup_dve")
        base_found = sem("base_found")
        key_rows = sem("key_rows")
        dst_rows = sem("dst_rows")
        src_rows = sem("src_rows")
        table_T = sem("table_T")
        table_out = sem("table_out")
        flags_made = sem("flags_made")
        blk_made = sem("blk_made")
        tables_stored = sem("tables_stored")
        blk_loaded = sem("blk_loaded")
        a_made = sem("a_made")
        aug_psum = sem("aug_psum")
        aug_ready = sem("aug_ready")
        phm_ready = sem("phm_ready")
        measured = sem("measured")
        normed = sem("normed")
        ln0_numbers = sem("ln0_numbers")
        ln0_h = sems("ln0_h", WXB)
        ln0_part = sem("ln0_part")
        ln0_sum = sems("ln0_sum", WXB)
        h_stored = sems("h_stored", WXB)
        mid_inv = sem("mid_inv")
        mid_agg = sem("mid_agg")
        mid_out = sem("mid_out")
        mid_numbers = sem("mid_numbers")
        mid_h = sem("mid_h")
        mid_hT_psum = sem("mid_hT_psum")
        mid_hT = sem("mid_hT")
        mid_wx_psum = sem("mid_wx_psum")
        mid_wx = sem("mid_wx")
        wx_stored = sems("wx_stored", WXB)
        pads_stored = sem("pads_stored")
        fin_num = sem("fin_num")
        fin_den = sem("fin_den")
        fin_psum = sem("fin_psum")
        fin_inv = sem("fin_inv")
        fin_y = sem("fin_y")
        fin_neg = sem("fin_neg")
        fin_exp = sem("fin_exp")
        fin_pos = sem("fin_pos")
        fin_out = sem("fin_out")
        out_stored = sems("out_stored", 2)

        def layer_sems(k):
            return dict(
                listed=sems(f"listed{k}_", 2),
                flagged=sems(f"flagged{k}_", 2),
                loaded=sems(f"loaded{k}_", (RING, 0)[k]),
                windowed=sems(f"windowed{k}_", (0, RING)[k]),
                gathered=sems(f"gathered{k}_", RING),
                msgT=sem(f"msgT{k}"),
                scored=sem(f"scored{k}"),
                scanned=sem(f"scanned{k}"),
                dropped=sem(f"dropped{k}"),
                shifted=sem(f"shifted{k}"),
                unturned=sem(f"unturned{k}"),
                weighed=sem(f"weighed{k}"),
                onehots=sem(f"onehots{k}"),
                onehotsT=sem(f"onehotsT{k}"),
                spread=sem(f"spread{k}"),
                targets=sem(f"targets{k}"),
                logits=sem(f"logits{k}"),
                multiplied=sem(f"multiplied{k}"),
                summed=sem(f"summed{k}"),
                merged=sem(f"merged{k}"),
                factored=sem(f"factored{k}"),
                acts=sem(f"acts{k}"),
            )

        L0, L1 = layer_sems(0), layer_sems(1)
        NE_DMA = 9
        W_DMA = 3 + 2 * PH + H

        self_res = sem("self_res")
        packed_ready = sem("packed_ready")

        def sweep_edges(eng, stages):
            sweep(eng, NG, RING, stages, reach=RING)

        block = ctx.enter_context(nc.Block())

        def offsets(eng, g):
            word = eng.value_load(packed[0:1, bass.ds(g, 1)], min_val=0, max_val=(WIN - P) * (1 + OFF + OFF * OFF))
            parts = (word % OFF, word // OFF % OFF, word // (OFF * OFF))
            return [0] + [nc.s_assert_within(eng.snap(x), 0, WIN - P, skip_runtime_bounds_check_because=
                                             "9 bits each, made by a min with WIN - P") for x in parts]

        @block.sync
        def _(sp):
            def rows(flat, lo, n):
                return flat[lo:lo + n * P].rearrange("(c e) -> c e", e=P)

            step = (NT - 1) // (LDX - 1)
            for k in range(LDX - 1):
                sp.dma_start(nodes[:, k * step:(k + 1) * step, :],
                             x_in[k * step * P:(k + 1) * step * P, :].rearrange("(t p) d -> p t d", p=P)
                             ).then_inc(x_loaded[k], 16)
            sp.wait_ge(node_pad, 1)
            sp.dma_start(nodes[0:LAST, NT - 1, :], x_in[(NT - 1) * P:N, :]).then_inc(x_loaded[LDX - 1], 16)
            sp.wait_ge(pads_in, 3)
            ct = CT - 1
            tail = FULL - ct * P
            for flat, tile in ((dst_in, dst_i), (src_in, src_i)):
                sp.dma_start(tile[:, 0:ct, :], flat[0:ct * P * P].rearrange("(t c e) -> c t e", c=P, e=P)
                             ).then_inc(edges_in, 16)
                sp.dma_start(tile[0:tail, ct, :], rows(flat, ct * P * P, tail)).then_inc(edges_in, 16)
                sp.dma_start(tile[tail:tail + 1, ct, 0:E - FULL * P],
                             flat[FULL * P:E].rearrange("(a e) -> a e", a=1)).then_inc(edges_in, 16)
            sp.dma_start(prev_i[0:1, 0, 1:P], dst_in[0:P - 1].rearrange("(a e) -> a e", a=1)).then_inc(edges_in, 16)
            sp.dma_start(prev_i[1:P, 0, :], rows(dst_in, P - 1, P - 1)).then_inc(edges_in, 16)
            sp.dma_start(prev_i[:, 1:ct, :], dst_in[P * P - 1:ct * P * P - 1].rearrange("(t c e) -> c t e", c=P, e=P)
                         ).then_inc(edges_in, 16)
            sp.dma_start(prev_i[0:tail, ct, :], rows(dst_in, ct * P * P - 1, tail)).then_inc(edges_in, 16)
            sp.dma_start(prev_i[tail:tail + 1, ct, 0:E - FULL * P + 1],
                         dst_in[FULL * P - 1:E].rearrange("(a e) -> a e", a=1)).then_inc(edges_in, 16)
            sp.dma_start(w1[:, :], w1_in).then_inc(weights_in, 16)
            sp.dma_start(bias_row[:, :], bias_in.rearrange("(a d) -> a d", a=1)).then_inc(weights_in, 16)
            sp.dma_start(beta[:, :], beta_in.rearrange("(a d) -> a d", a=1).to_broadcast([P, 1])).then_inc(weights_in, 16)
            for i in range(PH):
                part = slice(i * DB, (i + 1) * DB)
                sp.dma_start(rule_rep[part, :, :],
                             rule_in[:, i:i + 1, :].rearrange("n i j -> i n j").to_broadcast([DB, PH, PH])
                             ).then_inc(weights_in, 16)
                sp.dma_start(w0_rep[part, :, :], w0_in.rearrange("n a b -> a n b")).then_inc(weights_in, 16)
            for h in range(H):
                with nc.allow_non_contiguous_dma(reason="a vector of 32 numbers onto partitions"):
                    sp.dma_start(a_col[h * HD:(h + 1) * HD, :], a_in.rearrange("(k d) -> d k", k=2)
                                 ).then_inc(weights_in, 16)

            sp.wait_ge(const_ready, 1)
            sp.dma_start(wx_dram[N:N + WIN, :].rearrange("(t p) d -> p t d", p=P), msg[:, 0, :, :]
                         ).then_inc(pads_stored, 16)

            sp.wait_ge(flags_made, 1)
            sp.dma_start(flag_dram[0:ct * P * P].rearrange("(t c e) -> c t e", c=P, e=P), flag_b[:, 0:ct, :]
                         ).then_inc(tables_stored, 16)
            sp.dma_start(flag_dram[ct * P * P:NB * P + P].rearrange("(c e) -> c e", e=P),
                         flag_b[0:NB - ct * P + 1, ct, :]).then_inc(tables_stored, 16)
            sp.wait_ge(blk_made, 1)
            with nc.allow_non_contiguous_dma(reason="two numbers per block, from partitions to a row"):
                sp.dma_start(blk_dram.rearrange("k (t c) -> c k t", c=P), blk_i[:, :, :]).then_inc(tables_stored, 16)
            sp.wait_ge(tables_stored, 48)
            sp.dma_start(blk_row[:, :, :], blk_dram.rearrange("(a k) c -> a k c", a=1)).then_inc(blk_loaded, 16)

            def store_h(b, u, use):
                sp.wait_ge(ln0_h[u], use + 1)
                if isinstance(b, int) and b == NBAT - 1:
                    sp.dma_start(h_dram[b * GE:N, :], wgt[0:LAST, u, 0, :]).then_inc(h_stored[u], 16)
                else:
                    sp.dma_start(h_dram[bass.ds(b * GE, GE), :].rearrange("(t p) d -> p t d", p=P),
                                 wgt[:, u, :, :]).then_inc(h_stored[u], 16)

            sweep(sp, NBAT, WXB, [(0, store_h)])

            def load_lists(g, s, use, k):
                half = slice(s, s + HALF)
                if later(g, RING):
                    sp.wait_ge(k["onehots"], g - (RING - HALF))
                    apart(sp)
                    for q in range(s, s + HALF):
                        sp.wait_ge(k["gathered"][q], 64 * use)
                    apart(sp)
                sp.dma_start(meta_g[:, half, :], meta[:, bass.ds(g, HALF), :]).then_inc(k["listed"][s // HALF], 16)

            def load_flags(g, s, k, rows):
                if later(g, RING):
                    sp.wait_ge(k["dropped"], g - (RING - HALF))
                    apart(sp)
                run = flag_dram[bass.ds(g * GE, HALF * GE + 1)].rearrange("(a e) -> a e", a=1)
                sp.dma_start(flags[0:rows, s // HALF, :], run.to_broadcast([rows, HALF * GE + 1])
                             ).then_inc(k["flagged"][s // HALF], 16)

            def load0(g, s, use):
                if s % HALF == 0:
                    load_lists(g, s, use, L0)
                if later(g, RING):
                    sp.wait_ge(L0["multiplied"], g - (RING - 1))
                if isinstance(g, int) and (g + 1) * GE > E:
                    whole = (E - g * GE) // P
                    rest = E - g * GE - whole * P
                    if whole > 0:
                        sp.dma_start(msg[:, s, 0:whole, 0:D],
                                     ea_in[g * GE:g * GE + whole * P, :].rearrange("(b p) d -> p b d", p=P)
                                     ).then_inc(L0["loaded"][s], 16)
                    if rest > 0:
                        sp.dma_start(msg[0:rest, s, whole, 0:D], ea_in[E - rest:E, :]).then_inc(L0["loaded"][s], 16)
                else:
                    sp.dma_start(msg[:, s, :, 0:D],
                                 ea_in[bass.ds(g * GE, GE), :].rearrange("(b p) d -> p b d", p=P)
                                 ).then_inc(L0["loaded"][s], 16)

            sp.wait_ge(table_out, 2 * CT)
            def flags0(g, s, use):
                if s % HALF == 0:
                    load_flags(g, s, L0, P)

            sp.wait_ge(pads_stored, 16)
            sweep_edges(sp, [(0, load0), (1, flags0)])

            def store_wx(b, u, use):
                sp.wait_ge(mid_wx, b + 1)
                if isinstance(b, int) and b == NBAT - 1:
                    sp.dma_start(wx_dram[b * GE:N, :], msg[0:LAST, u, 0, :]).then_inc(wx_stored[u], 16)
                else:
                    sp.dma_start(wx_dram[bass.ds(b * GE, GE), :].rearrange("(t p) d -> p t d", p=P),
                                 msg[:, u, :, :]).then_inc(wx_stored[u], 16)

            sweep(sp, NBAT, WXB, [(0, store_wx)])
            sp.wait_ge(packed_ready, 1)

            def load1(g, s, use):
                if s % HALF == 0:
                    load_lists(g, s, use, L1)
                if isinstance(g, int) and g == 0:
                    for u in range(WXB):
                        sp.wait_ge(wx_stored[u], 16 * ((NBAT - 1 - u) // WXB + 1))
                if later(g, RING):
                    sp.wait_ge(L1["targets"], g - (RING - 1))
                first = sp.value_load(blk_row[0:1, 1, bass.ds(g * GB, 1)], min_val=0, max_val=N - 1)
                offset = offsets(sp, g)
                for b in range(GB):
                    sp.dma_start(window[:, s, b, :], wx_dram[bass.ds(first + offset[b], P), D + H:TW]).then_inc(L1["windowed"][s], 16)

            def flags1(g, s, use):
                if s % HALF == 0:
                    load_flags(g, s, L1, H)

            sweep_edges(sp, [(0, load1), (2, flags1)])

            def store_out(b, u, use):
                sp.wait_ge(fin_out, b + 1)
                if isinstance(b, int) and b == NBAT - 1:
                    sp.dma_start(out[b * GE:N, :], fin[0:LAST, u, 0:D]).then_inc(out_stored[u], 16)
                else:
                    sp.dma_start(out[bass.ds(b * GE, GE), :].rearrange("(t p) d -> p t d", p=P),
                                 fin[:, u, :].rearrange("p (t d) -> p t d", d=D)).then_inc(out_stored[u], 16)

            sweep(sp, NBAT, 2, [(0, store_out)])
            for u in range(2):
                sp.wait_ge(out_stored[u], 16 * ((NBAT + 1 - u) // 2))

        def loads0(g):
            if (g + 1) * GE <= E:
                return 1
            left = max(E - g * GE, 0)
            return (left >= P) + (left % P > 0)

        @block.gpsimd
        def _(pool):
            pool.memset(dst_i[:, CT - 1, :], NOWHERE).then_inc(pads_in, 1)
            pool.memset(prev_i[:, :, :], NOWHERE).then_inc(pads_in, 1)
            pool.memset(src_i[:, CT - 1, :], 0).then_inc(pads_in, 1)
            pool.memset(ident[:, :], 0.0).then_inc(self_pool, 1)
            pool.memset(group_pick[:, :], 0.0).then_inc(self_pool, 1)
            pool.memset(head_mask[:, :], 1.0).then_inc(self_pool, 1)
            pool.memset(head_spread[:, :], 1.0).then_inc(self_pool, 1)
            pool.memset(head_pick[:, :], 0.0).then_inc(self_pool, 1)
            pool.wait_ge(self_pool, 5)
            pool.affine_select(out=ident[:, :], in_=ident[:, :], pattern=[[-1, P]], compare_op=ALU.not_equal,
                               fill=1.0, base=0, channel_multiplier=1).then_inc(self_pool, 1)
            pool.affine_select(out=group_pick[:, :].rearrange("p (g b) -> p g b", b=GB),
                               in_=group_pick[:, :].rearrange("p (g b) -> p g b", b=GB),
                               pattern=[[-GB, P // GB], [0, GB]], compare_op=ALU.not_equal,
                               fill=1.0, base=0, channel_multiplier=1).then_inc(self_pool, 1)
            pool.affine_select(out=head_pick[:, :], in_=head_pick[:, :], pattern=[[-HD, H]], compare_op=ALU.not_equal,
                               fill=1.0, base=0, channel_multiplier=1).then_inc(self_pool, 1)
            pool.affine_select(out=head_mask[:, :], in_=head_mask[:, :], pattern=[[-HD, H]], compare_op=ALU.is_ge,
                               fill=0.0, base=0, channel_multiplier=1).then_inc(self_pool, 1)
            pool.affine_select(out=head_spread[:, :], in_=head_spread[:, :], pattern=[[1, D]], compare_op=ALU.is_ge,
                               fill=0.0, base=0, channel_multiplier=-HD).then_inc(self_pool, 1)
            pool.wait_ge(self_pool, 10)
            pool.affine_select(out=head_mask[:, :], in_=head_mask[:, :], pattern=[[HD, H]], compare_op=ALU.is_ge,
                               fill=0.0, base=HD - 1, channel_multiplier=-1).then_inc(self_pool, 1)
            pool.affine_select(out=head_spread[:, :], in_=head_spread[:, :], pattern=[[-1, D]], compare_op=ALU.is_ge,
                               fill=0.0, base=HD - 1, channel_multiplier=HD).then_inc(self_pool, 1)
            pool.iota(iota_i[:, :], pattern=[[1, P]], base=0, channel_multiplier=0).then_inc(self_pool, 1)
            pool.wait_ge(self_pool, 13)
            pool.tensor_copy(iota_f[:, :], iota_i[:, :]).then_inc(self_pool, 1)
            pool.memset(ones_row[:, :], 1.0).then_inc(self_pool, 1)
            pool.memset(zero_row[:, :], 0.0).then_inc(self_pool, 1)
            pool.memset(msg[:, :, :, :], 0.0).then_inc(self_pool, 1)
            pool.wait_ge(self_pool, 17)
            pool.memset(junk[:, :], 0.0).then_inc(const_ready, 1)

            def batch_numbers(b, u, done):
                n = 1 if isinstance(b, int) and b == NBAT - 1 else GB
                apart(pool)
                pool.tensor_copy(norm_b[:, u, :, 0:n], norm[:, :, bass.ds(b * GB, n)]).then_inc(done, 1)

            def numbers0(b, u, use):
                if later(b, WXB):
                    pool.wait_ge(ln0_h[u], use)
                batch_numbers(b, u, ln0_numbers)

            def residual(b, u, use):
                if u not in DVE_SLOTS:
                    pool.wait_ge(ln0_h[u], use + 1)
                    apart(pool)
                    last = isinstance(b, int) and b == NBAT - 1
                    t = GB if not last else 1
                    tiles = nodes[:, bass.ds(b * GB, t), :] if not last else nodes[:, b * GB:b * GB + 1, :]
                    pool.tensor_tensor(tiles, tiles, wgt[:, u, 0:t, :], ALU.add).then_inc(ln0_sum[u], 1)

            pool.wait_ge(normed, 1)
            sweep(pool, NBAT, WXB, [(0, numbers0), (2, residual)])
            for u in range(WXB):
                pool.wait_ge(h_stored[u], 16 * ((NBAT - 1 - u) // WXB + 1))

            def gather0(g, s, use):
                base = sum(loads0(q) for q in range(s, min(g, NG) if isinstance(g, int) else 0, RING))
                want = 16 * (base + loads0(g)) if isinstance(g, int) else 16 * (use + 1)
                pool.wait_ge(L0["listed"][s // HALF], 16 * (use + 1))
                pool.wait_ge(L0["loaded"][s], want)
                apart(pool)
                for b in range(GB):
                    pool.indirect_dma_start(msg[:, s, b, 0:D], None, h_dram,
                                            bass.IndirectOffsetOnAxis(ap=meta_g[:, s, b:b + 1], axis=0),
                                            compute_op=ALU.add).then_inc(L0["gathered"][s], 16)

            sweep_edges(pool, [(0, gather0)])

            def numbers1(b, u, use):
                if later(b, 2):
                    pool.wait_ge(mid_h, b - 1)
                batch_numbers(b, u, mid_numbers)

            def average0(b, u, use):
                w = LAST if isinstance(b, int) and b == NBAT - 1 else GE
                pool.wait_ge(mid_inv, b + 1)
                if later(b, 2):
                    pool.wait_ge(mid_out, b - 1)
                apart(pool)
                pool.tensor_tensor(aggT[:, u, 0:w], acc[:, 0, bass.ds(b * GE, w)], inv[:, u, 0:w], ALU.mult
                                   ).then_inc(mid_agg, 1)

            sweep(pool, NBAT, 2, [(1, average0)])
            pool.wait_ge(normed, 2)
            sweep(pool, NBAT, 2, [(0, numbers1)])

            def gather1(g, s, use):
                pool.wait_ge(L1["listed"][s // HALF], 16 * (use + 1))
                if later(g, RING):
                    pool.wait_ge(L1["multiplied"], g - (RING - 1))
                apart(pool)
                for b in range(GB):
                    pool.indirect_dma_start(msg[:, s, b, :], None, wx_dram,
                                            bass.IndirectOffsetOnAxis(ap=meta_g[:, s, b:b + 1], axis=0)
                                            ).then_inc(L1["gathered"][s], 16)

            for u in range(WXB):
                pool.wait_ge(wx_stored[u], 16 * ((NBAT - 1 - u) // WXB + 1))
            sweep_edges(pool, [(0, gather1)])

            def denominators(b, u, use):
                if later(b, 2):
                    pool.wait_ge(fin_psum, b - 1)
                apart(pool)
                w = LAST if isinstance(b, int) and b == NBAT - 1 else GE
                pool.tensor_copy(hT[:, u, 0:w], acc[:, 1, bass.ds(b * GE, w)]).then_inc(fin_den, 1)

            pool.wait_ge(L1["merged"], NG)
            sweep(pool, NBAT, 2, [(0, denominators)])

        @block.scalar
        def _(act):
            def h0(b, u, use):
                if u not in DVE_SLOTS:
                    act.wait_ge(ln0_numbers, b + 1)
                    if later(b, WXB):
                        act.wait_ge(h_stored[u], 16 * use)
                        act.wait_ge(ln0_sum[u], use)
                    apart(act)
                    for t in range(1 if isinstance(b, int) and b == NBAT - 1 else GB):
                        ins = act.activation(wgt[:, u, t, :], nodes[:, bass.ds(b * GB + t, 1), :].rearrange("p a d -> p (a d)"),
                                             ACT.Relu, bias=norm_b[:, u, 1, t:t + 1], scale=norm_b[:, u, 0, t:t + 1])
                    ins.then_inc(ln0_h[u], 1)

            act.wait_ge(const_ready, 1)
            meta_t = meta[:, :, :].rearrange("p (t g) k -> p t g k", t=CT)
            for t in range(CT):
                act.wait_ge(table_T, 2 * t + 1)
                act.activation(meta_t[:, t, :, 0:GB], bank[2][:, 0:P].rearrange("p (g b) -> p g b", b=GB), ACT.Copy
                               ).then_inc(table_out, 1)
                act.wait_ge(table_T, 2 * t + 2)
                act.activation(meta_t[:, t, :, GB:2 * GB].bitcast(F32), bank[3][:, 0:P].rearrange("p (g b) -> p g b", b=GB),
                               ACT.Copy).then_inc(table_out, 1)
            sweep(act, NBAT, WXB, [(0, h0)])

            def merge(g, s, use, k, read_out):
                par = s % 2
                act.wait_ge(k["summed"], g + 1)
                if isinstance(g, int) and g == 0:
                    if read_out is not None:
                        act.wait_ge(read_out, NBAT)
                    act.activation(acc[:, :, 0:WIN], sums[:, par, :, :], ACT.Copy).then_inc(k["merged"], 1)
                    return
                node = act.value_load(blk_row[0:1, 1, bass.ds(g * GB, 1)], min_val=0, max_val=N - 1)
                act.wait_ge(k["factored"], g + 1)
                act.wait_ge(k["merged"], g)
                apart(act)
                act.activation(carried[:, :], acc[:, :, bass.ds(node, 1)].rearrange("p k a -> p (k a)"), ACT.Copy,
                               scale=scale[:, s:s + 1]).then_inc(k["acts"], 1)
                act.wait_ge(k["acts"], g)
                apart(act)
                act.activation(acc[:, 0, bass.ds(node, 1)], sums[:, par, 0, 0:1], ACT.Identity,
                               bias=carried[:, 0:1])
                act.activation(acc[:, 1, bass.ds(node, 1)], sums[:, par, 1, 0:1], ACT.Identity,
                               bias=carried[:, 1:2])
                act.activation(acc[:, :, bass.ds(node + 1, WIN - 1)], sums[:, par, :, 1:WIN], ACT.Copy
                               ).then_inc(k["merged"], 1)

            act.wait_ge(weights_in, 16 * W_DMA)
            act.wait_ge(blk_loaded, 16)

            for u in range(WXB):
                if u not in DVE_SLOTS:
                    act.wait_ge(ln0_sum[u], (NBAT - 1 - u) // WXB + 1)

            def score0(g, s, use):
                act.wait_ge(L0["msgT"], g + 1)
                if later(g, 2):
                    act.wait_ge(L0["shifted"], g - 1)
                act.activation(score[:, s % 2, :], bank[s % 2][:, :], ACT.Copy, scale=beta[:, 0:1]
                               ).then_inc(L0["scored"], 1)

            def weigh0(g, s, use):
                act.wait_ge(L0["unturned"], g + 1)
                if later(g, WGT):
                    act.wait_ge(L0["summed"], g - (WGT - 1))
                act.activation(wgt[:, s % WGT, :, :], bank[2 + s % 2][:, :].rearrange("p (b d) -> p b d", b=GB), ACT.Exp
                               ).then_inc(L0["weighed"], 1)
                act.wait_ge(L0["dropped"], g + 1)
                act.activation(scale[:, s:s + 1], drop[:, s:s + 1], ACT.Exp).then_inc(L0["factored"], 1)

            def merge0(g, s, use):
                merge(g, s, use, L0, None)

            sweep_edges(act, [(5, merge0), (0, score0), (2, weigh0)])

            def h1(b, u, use):
                act.wait_ge(mid_numbers, b + 1)
                if later(b, 2):
                    act.wait_ge(mid_hT_psum, b - 1)
                apart(act)
                for t in range(1 if isinstance(b, int) and b == NBAT - 1 else GB):
                    ins = act.activation(hn[:, u, t, :], nodes[:, bass.ds(b * GB + t, 1), :].rearrange("p a d -> p (a d)"),
                                         ACT.Relu, bias=norm_b[:, u, 1, t:t + 1], scale=norm_b[:, u, 0, t:t + 1])
                ins.then_inc(mid_h, 1)

            sweep(act, NBAT, 2, [(0, h1)])

            def weigh1(g, s, use):
                act.wait_ge(L1["shifted"], g + 1)
                if later(g, WGT):
                    act.wait_ge(L1["summed"], g - (WGT - 1))
                act.activation(wgt[:, s % WGT, :, :].rearrange("p b (h d) -> p (b h) d", h=H),
                               logit_d[:, s % 2, :].rearrange("p (k a) -> p k a", a=1).to_broadcast([P, GB * H, HD]),
                               ACT.Exp).then_inc(L1["weighed"], 1)
                act.activation(scale[:, s:s + 1], bank[3][:, 64 + s:65 + s], ACT.Exp).then_inc(L1["factored"], 1)

            def spread1(g, s, use):
                act.wait_ge(L1["onehotsT"], g + 1)
                if later(g, 2):
                    act.wait_ge(L1["targets"], g - 1)
                act.activation(onehotT[:, s % 2, :], bank[0][:, :], ACT.Copy).then_inc(L1["spread"], 1)

            def merge1(g, s, use):
                merge(g, s, use, L1, mid_agg)

            sweep_edges(act, [(5, weigh1), (1, spread1), (8, merge1)])

            def elu(b, u, use):
                act.wait_ge(fin_y, b + 1)
                if later(b, 2):
                    act.wait_ge(fin_out, b - 1)
                w = D if isinstance(b, int) and b == NBAT - 1 else GE
                r = LAST if isinstance(b, int) and b == NBAT - 1 else P
                act.activation(elu_e[0:r, u, 0:w], aggT[0:r, u, 0:w], ACT.Relu, scale=-1.0).then_inc(fin_neg, 1)
                act.wait_ge(fin_neg, b + 1)
                act.activation(elu_e[0:r, u, 0:w], elu_e[0:r, u, 0:w], ACT.Exp, scale=-1.0).then_inc(fin_exp, 1)

            def numerators(b, u, use):
                if later(b, 2):
                    act.wait_ge(fin_psum, b - 1)
                apart(act)
                w = LAST if isinstance(b, int) and b == NBAT - 1 else GE
                act.activation(hn_row[:, u, 0:w], acc[:, 0, bass.ds(b * GE, w)], ACT.Copy).then_inc(fin_num, 1)

            act.wait_ge(L1["merged"], NG)
            sweep(act, NBAT, 2, [(2, elu), (0, numerators)])

        @block.vector
        def _(dve):
            dve.memset(nodes[:, NT - 1, :], 0.0).then_inc(node_pad, 1)

            links = [0]

            def link(ins):
                links[0] += 1
                ins.then_inc(setup_dve, 1)
                dve.wait_ge(setup_dve, links[0])

            def statistics(b):
                apart(dve)
                for t in range(1 if isinstance(b, int) and b == NBAT - 1 else GB):
                    ins = dve.bn_stats(stats[:, bass.ds(b * GB + t, 1), :].rearrange("p a k -> p (a k)"),
                                       nodes[:, bass.ds(b * GB + t, 1), :].rearrange("p a d -> p (a d)"))
                ins.then_inc(measured, 1)

            def norm_all_nodes():
                y, t, v = norm[:, 0, :], newton[:, :], spread_v[:, :]
                link(dve.tensor_tensor(t, stats[:, :, 1], stats[:, :, 4], ALU.subtract))
                link(dve.scalar_tensor_tensor(y, t, 0.25, t, ALU.mult, ALU.mult))
                link(dve.tensor_tensor(v, stats[:, :, 2], stats[:, :, 5], ALU.add))
                link(dve.scalar_tensor_tensor(v, v, 1.0 / D, y, ALU.mult, ALU.add))
                link(dve.tensor_tensor(mean_2[:, :], stats[:, :, 1], stats[:, :, 4], ALU.add))
                link(dve.tensor_scalar(v, v, EPS, None, ALU.add))
                link(dve.tensor_scalar(t.bitcast(I32), v.bitcast(I32), 1, None, ALU.logical_shift_right))
                link(dve.tensor_scalar(y.bitcast(I32), t.bitcast(I32), -1, 0x5F3759DF, ALU.mult, ALU.add))
                for step in range(3):
                    link(dve.tensor_tensor(t, y, y, ALU.mult))
                    link(dve.tensor_tensor(t, t, v, ALU.mult))
                    link(dve.tensor_scalar(t, t, -0.5, 1.5, ALU.mult, ALU.add))
                    link(dve.tensor_tensor(y, y, t, ALU.mult))
                dve.scalar_tensor_tensor(norm[:, 1, :], mean_2[:, :], -0.5, y, ALU.mult, ALU.mult).then_inc(normed, 1)

            per = (NT - 1) // (LDX - 1) // GB
            half = (LDX - 1) // 2
            for k in range(half):
                dve.wait_ge(x_loaded[k], 16)
                with dve.Fori(k * per, (k + 1) * per) as b:
                    statistics(b)

            dve.wait_ge(edges_in, 16 * (NE_DMA + 2))
            dve.tensor_copy(dst_f[:, :, :], dst_i[:, :, :]).then_inc(dst_rows, 1)
            dve.tensor_copy(src_f[:, :, :], src_i[:, :, :]).then_inc(src_rows, 1)
            dve.wait_ge(dst_rows, 1)
            dve.wait_ge(base_found, 1)
            link(dve.tensor_tensor(start_f[:, :, 0], dst_f[:, :, 0], bank[0][:, 0:CT], ALU.subtract))
            link(dve.tensor_scalar(blk_f[:, :, 0], start_f[:, :, 0], 0.0, float(WIN - P), ALU.max, ALU.min))
            link(dve.tensor_copy(blk_f[:, :, 1], bank[0][:, 0:CT]))
            link(dve.tensor_tensor(blk_f[:, :, 2], blk_f[:, :, 0], blk_f[:, :, 1], ALU.add))
            dve.tensor_copy(blk_i[:, 0, :], blk_f[:, :, 0])
            dve.tensor_copy(blk_i[:, 1, :], blk_f[:, :, 2]).then_inc(blk_made, 1)
            link(dve.tensor_tensor(start_f[:, :, :], dst_i[:, :, :], prev_i[:, :, :], ALU.not_equal))
            dve.tensor_scalar(flag_b[:, :, :], start_f[:, :, :], -BIG, None, ALU.mult).then_inc(flags_made, 1)
            dve.tensor_tensor(dst_f[:, :, :], dst_f[:, :, :], blk_f[:, :, 2:3].to_broadcast([P, CT, P]), ALU.subtract
                              ).then_inc(key_rows, 1)
            for k in range(half, LDX - 1):
                dve.wait_ge(x_loaded[k], 16)
                with dve.Fori(k * per, (k + 1) * per) as b:
                    statistics(b)
            dve.wait_ge(x_loaded[LDX - 1], 16)
            statistics(NBAT - 1)
            dve.wait_ge(measured, NBAT)
            norm_all_nodes()

            def h0(b, u, use):
                if u in DVE_SLOTS:
                    dve.wait_ge(ln0_numbers, b + 1)
                    if later(b, WXB):
                        dve.wait_ge(h_stored[u], 16 * use)
                    made = use * len(DVE_SLOTS) + DVE_SLOTS.index(u)
                    if later(b, 2):
                        dve.wait_ge(ln0_part, 3 * made)
                    apart(dve)
                    for t in range(GB):
                        ins = dve.tensor_scalar(run_max[:, 0, t * D:(t + 1) * D],
                                                nodes[:, bass.ds(b * GB + t, 1), :].rearrange("p a d -> p (a d)"),
                                                norm_b[:, u, 0, t:t + 1], norm_b[:, u, 1, t:t + 1], ALU.mult, ALU.add)
                    ins.then_inc(ln0_part, 1)
                    dve.wait_ge(ln0_part, 3 * made + 1)
                    lnx = run_max[:, 0, :].rearrange("p (t d) -> p t d", d=D)
                    dve.tensor_scalar(wgt[:, u, :, :], lnx, 0.0, None, ALU.max).then_inc(ln0_h[u], 1)
                    tiles = nodes[:, bass.ds(b * GB, GB), :]
                    dve.scalar_tensor_tensor(tiles, lnx, 0.0, tiles, ALU.max, ALU.add).then_inc(ln0_part, 2)

            sweep(dve, NBAT, WXB, [(0, h0)])

            dve.wait_ge(blk_loaded, 16)
            off_b = blk_row[0:1, 0, :].rearrange("a (g b) -> a g b", b=GB)
            link(dve.tensor_scalar(packed[:, :], off_b[:, :, 3], 9, None, ALU.logical_shift_left))
            link(dve.tensor_tensor(packed[:, :], packed[:, :], off_b[:, :, 2], ALU.bitwise_or))
            link(dve.tensor_scalar(part[:, :], packed[:, :], 9, None, ALU.logical_shift_left))
            dve.tensor_tensor(packed[:, :], part[:, :], off_b[:, :, 1], ALU.bitwise_or).then_inc(packed_ready, 1)
            dve.wait_ge(weights_in, 16 * W_DMA)
            for n in range(PH):
                left = rule_rep[:, n, :].rearrange("p (j a) -> p j a", a=1).to_broadcast([P, PH, DB])
                right = w0_rep[:, n:n + 1, :].to_broadcast([P, PH, DB])
                link(dve.tensor_tensor((phm if n == 0 else phm_term)[:, :, :], left, right, ALU.mult))
                if n:
                    link(dve.tensor_tensor(phm[:, :, :], phm[:, :, :], phm_term[:, :, :], ALU.add))
            dve.sem_inc(phm_ready, 1)
            for j in range(2):
                ins = dve.tensor_scalar(a_heads[:, j * H:(j + 1) * H], head_mask[:, :], a_col[:, j:j + 1], None, ALU.mult)
            ins.then_inc(a_made, 1)
            dve.wait_ge(aug_psum, 1)
            dve.tensor_copy(w1_aug[:, 0:D], bank[0][:, 0:D])
            dve.tensor_copy(w1_aug[:, D:TW], bank[0][:, D:TW]).then_inc(aug_ready, 1)

            def one_hot(g, s, use, k):
                if later(g, RING):
                    dve.wait_ge(k["summed"], g - (RING - 1))
                dve.wait_ge(k["listed"][s // HALF], 16 * (use + 1))
                key = meta_g[:, s, GB:2 * GB].bitcast(F32)
                for b in range(GB):
                    ins = dve.tensor_scalar(onehot[:, s, b, :], iota_f[:, :], key[:, b:b + 1], None, ALU.is_equal)
                ins.then_inc(k["onehots"], 1)

            def segment_max(g, s, use, k, n, data):
                par = s % 2
                lo = s % HALF * GE
                flag = flags[0:n, s // HALF, lo:lo + GE + 1]
                dve.wait_ge(k["flagged"][s // HALF], 16 * (use + 1))
                if isinstance(g, int) and g == 0:
                    before = -BIG
                else:
                    dve.wait_ge(k["dropped"], g)
                    before = run_max[0:n, 1 - par, GE - 1:GE]
                dve.tensor_tensor_scan(run_max[0:n, par, :], flag[:, 0:GE], data, before, ALU.add, ALU.max
                                       ).then_inc(k["scanned"], 1)
                dve.wait_ge(k["scanned"], 2 * g + 1)
                dve.tensor_tensor_scan(seg_max[0:n, par, ::-1], flag[:, GE:0:-1], run_max[0:n, par, ::-1], -BIG,
                                       ALU.add, ALU.max).then_inc(k["scanned"], 1)
                dve.wait_ge(k["scanned"], 2 * g + 2)
                if not (isinstance(g, int) and g == 0):
                    if later(g, RING):
                        dve.wait_ge(k["factored"], g - (RING - 1))
                    dve.scalar_tensor_tensor(drop[0:n, s:s + 1], run_max[0:n, 1 - par, GE - 1:GE], seg_max[0:n, par, 0:1],
                                             flag[:, 0:1], ALU.subtract, ALU.add).then_inc(k["dropped"], 1)
                else:
                    dve.memset(drop[0:n, s:s + 1], 0.0).then_inc(k["dropped"], 1)

            def maxima0(g, s, use):
                par = s % 2
                dve.wait_ge(L0["scored"], g + 1)
                segment_max(g, s, use, L0, P, score[:, par, :])
                if later(g, 2):
                    dve.wait_ge(L0["unturned"], g - 1)
                dve.tensor_tensor(diff[:, par, :], score[:, par, :], seg_max[:, par, :], ALU.subtract
                                  ).then_inc(L0["shifted"], 1)

            def products(g, s, use, k):
                par = s % 2
                if later(g, 2):
                    dve.wait_ge(k["summed"], g - 1)
                dve.wait_ge(k["weighed"], g + 1)
                dve.tensor_tensor(prod[:, par, :, :], wgt[:, s % WGT, :, :], msg[:, s, :, 0:D], ALU.mult
                                  ).then_inc(k["multiplied"], 1)


            def products0(g, s, use):
                products(g, s, use, L0)

            def one_hot0(g, s, use):
                one_hot(g, s, use, L0)

            sweep_edges(dve, [(0, one_hot0), (1, maxima0), (3, products0)])

            dve.wait_ge(L0["merged"], NG)

            def invert0(b, u, use):
                w = LAST if isinstance(b, int) and b == NBAT - 1 else GE
                if later(b, 2):
                    dve.wait_ge(mid_agg, b - 1)
                dve.reciprocal(inv[:, u, 0:w], acc[:, 1, bass.ds(b * GE, w)]).then_inc(mid_inv, 1)

            def finish0(b, u, use):
                last = isinstance(b, int) and b == NBAT - 1
                t = 1 if last else GB
                rows = LAST if last else P
                dve.wait_ge(mid_out, b + 1)
                tiles = nodes[0:rows, b * GB:b * GB + 1, :] if last else nodes[:, bass.ds(b * GB, GB), :]
                dve.tensor_tensor(tiles, tiles, sums[0:rows, u, 0, 0:t * D].rearrange("p (t d) -> p t d", d=D), ALU.add
                                  ).then_inc(self_res, 1)
                dve.wait_ge(self_res, b + 1)
                statistics(b)

            for u in range(WXB):
                if u not in DVE_SLOTS:
                    dve.wait_ge(ln0_sum[u], (NBAT - 1 - u) // WXB + 1)
            sweep(dve, NBAT, 2, [(3, finish0), (0, invert0)])
            dve.wait_ge(measured, 2 * NBAT)
            norm_all_nodes()

            def hT1(b, u, use):
                dve.wait_ge(mid_hT_psum, b + 1)
                if later(b, 2):
                    dve.wait_ge(mid_wx_psum, b - 1)
                w = P if isinstance(b, int) and b == NBAT - 1 else GE
                dve.tensor_copy(hT[:, u % 2, 0:w], bank[u % 2][:, 0:w]).then_inc(mid_hT, 1)

            def wx1(b, u, use):
                dve.wait_ge(mid_wx_psum, b + 1)
                if later(b, WXB):
                    dve.wait_ge(wx_stored[u], 16 * use)
                if not (isinstance(b, int) and b == NBAT - 1):
                    dve.tensor_copy(msg[:, u, IN_BANK, :], sums[:, u % 2, 1, 0:TW])
                t = 1 if isinstance(b, int) and b == NBAT - 1 else IN_BANK
                dve.tensor_copy(msg[:, u, 0:t, :], bank[2 + u % 2][:, 0:t * TW].rearrange("p (t d) -> p t d", d=TW)
                                ).then_inc(mid_wx, 1)

            sweep(dve, NBAT, WXB, [(1, hT1), (3, wx1)])

            def one_hot1(g, s, use):
                one_hot(g, s, use, L1)

            def logits1(g, s, use):
                dve.wait_ge(L1["gathered"][s], 64 * (use + 1))
                dve.wait_ge(L1["targets"], g + 1)
                if later(g, 1):
                    dve.wait_ge(L1["logits"], 2 * g)
                dve.tensor_tensor(logit_v[:, :].rearrange("p (b h) -> p b h", h=H),
                                  bank[2][:, 0:GB * H].rearrange("p (b h) -> p b h", h=H),
                                  msg[:, s, :, D:D + H], ALU.add).then_inc(L1["logits"], 1)
                dve.wait_ge(L1["logits"], 2 * g + 1)
                dve.scalar_tensor_tensor(logit[:, s % WGT, :], logit_v[:, :], 0.2, logit_v[:, :], ALU.mult, ALU.max
                                         ).then_inc(L1["logits"], 1)

            def maxima1(g, s, use):
                dve.wait_ge(L1["msgT"], g + 1)
                segment_max(g, s, use, L1, H, bank[1][0:H, :])

            def shift1(g, s, use):
                dve.wait_ge(L1["unturned"], g + 1)
                if later(g, 2):
                    dve.wait_ge(L1["weighed"], g - 1)
                dve.tensor_tensor(logit_d[:, s % 2, :], logit[:, s % WGT, :], bank[3][:, 0:GB * H], ALU.subtract
                                  ).then_inc(L1["shifted"], 1)

            def products1(g, s, use):
                products(g, s, use, L1)

            sweep_edges(dve, [(3, logits1), (5, shift1), (4, maxima1), (0, one_hot1), (6, products1)])

            def divide(b, u, use):
                last = isinstance(b, int) and b == NBAT - 1
                t = 1 if last else GB
                w, r = t * D, (LAST if last else P)
                dve.wait_ge(fin_psum, b + 1)
                if later(b, 1):
                    dve.wait_ge(fin_y, b)
                dve.reciprocal(inv_head[0:r, 0:t * H], bank[2 + u][0:r, 0:t * H]).then_inc(fin_inv, 1)
                if later(b, 2):
                    dve.wait_ge(fin_exp, b - 1)
                    dve.wait_ge(fin_pos, b - 1)
                dve.wait_ge(fin_inv, b + 1)
                dve.tensor_tensor(aggT[0:r, u, 0:w].rearrange("p (k d) -> p k d", d=HD),
                                  bank[u][0:r, 0:w].rearrange("p (k d) -> p k d", d=HD),
                                  inv_head[0:r, 0:t * H].rearrange("p (k a) -> p k a", a=1).to_broadcast([r, t * H, HD]),
                                  ALU.mult).then_inc(fin_y, 1)

            def finish1(b, u, use):
                last = isinstance(b, int) and b == NBAT - 1
                t = 1 if last else GB
                w, r = t * D, (LAST if last else P)
                tiles = nodes[:, b * GB:b * GB + 1, :] if last else nodes[:, bass.ds(b * GB, GB), :]
                if later(b, 2):
                    dve.wait_ge(fin_out, b - 1)
                dve.wait_ge(fin_y, b + 1)
                dve.scalar_tensor_tensor(pos[0:r, u, 0:w].rearrange("p (t d) -> p t d", d=D),
                                         aggT[0:r, u, 0:w].rearrange("p (t d) -> p t d", d=D), 0.0, tiles[0:r],
                                         ALU.max, ALU.add).then_inc(fin_pos, 1)
                dve.wait_ge(fin_pos, b + 1)
                dve.wait_ge(fin_exp, b + 1)
                if later(b, 2):
                    dve.wait_ge(out_stored[u], 16 * use)
                dve.scalar_tensor_tensor(fin[0:r, u, 0:w], elu_e[0:r, u, 0:w], -1.0, pos[0:r, u, 0:w], ALU.add, ALU.add
                                         ).then_inc(fin_out, 1)

            sweep(dve, NBAT, 2, [(1, divide), (2, finish1)])

        @block.tensor
        def _(pe):
            pe.wait_ge(const_ready, 1)
            pe.wait_ge(dst_rows, 1)
            pe.matmul(bank[0][:, 0:CT], group_pick[:, :], dst_f[:, :, 0], start=True, stop=True).then_inc(base_found, 1)
            pe.wait_ge(src_rows, 1)
            pe.wait_ge(key_rows, 1)
            for t in range(CT):
                if t:
                    pe.wait_ge(table_out, 2 * t - 1)
                pe.transpose(bank[2][:, 0:P], src_f[:, t, :], ident[:, :]).then_inc(table_T, 1)
                if t:
                    pe.wait_ge(table_out, 2 * t)
                pe.transpose(bank[3][:, 0:P], dst_f[:, t, :], ident[:, :]).then_inc(table_T, 1)
            pe.wait_ge(weights_in, 16 * W_DMA)
            pe.wait_ge(a_made, 1)
            pe.transpose(bank[0][:, 0:D], w1[:, :], ident[:, :])
            pe.matmul(bank[0][:, D:TW], w1[:, :], a_heads[:, :], start=True, stop=True).then_inc(aug_psum, 1)
            pe.wait_ge(aug_ready, 1)
            pe.wait_ge(packed_ready, 1)

            for par in range(2):
                for j in range(2):
                    ins = pe.matmul(sums[:, par, j, :], zero_row[0:1, 0:P], zero_row[0:1, :], start=True, stop=True)

            def segment_sums(g, s, k):
                par = s % 2
                pe.wait_ge(k["onehots"], g + 1)
                pe.wait_ge(k["multiplied"], g + 1)
                if later(g, 2):
                    pe.wait_ge(k["merged"], g - 1)
                offset = offsets(pe, g)
                for b in range(GB):
                    off = offset[b]
                    for j, (what, slot) in enumerate(((prod, par), (wgt, s % WGT))):
                        ins = pe.matmul(sums[:, par, j, bass.ds(off, P)], what[:, slot, b, :], onehot[:, s, b, :],
                                        start=(b == 0), stop=(b == GB - 1), skip_group_check=True)
                ins.then_inc(k["summed"], 1)

            def turn0(g, s, use):
                pe.wait_ge(L0["gathered"][s], 64 * (use + 1))
                if later(g, 2):
                    pe.wait_ge(L0["scored"], g - 1)
                for b in range(GB):
                    ins = pe.transpose(bank[s % 2][:, b * P:(b + 1) * P], msg[:, s, b, 0:D], ident[:, :])
                ins.then_inc(L0["msgT"], 1)

            def unturn0(g, s, use):
                pe.wait_ge(L0["shifted"], g + 1)
                if later(g, 2):
                    pe.wait_ge(L0["weighed"], g - 1)
                for b in range(GB):
                    ins = pe.transpose(bank[2 + s % 2][:, b * P:(b + 1) * P], diff[:, s % 2, b * P:(b + 1) * P], ident[:, :])
                ins.then_inc(L0["unturned"], 1)

            def sums0(g, s, use):
                segment_sums(g, s, L0)

            sweep_edges(pe, [(4, sums0), (0, turn0), (2, unturn0)])

            pe.wait_ge(phm_ready, 1)

            def layer_out(b, u, use):
                last = isinstance(b, int) and b == NBAT - 1
                pe.wait_ge(mid_agg, b + 1)
                if later(b, 2):
                    pe.wait_ge(self_res, b - 1)
                elif b == 0:
                    pe.wait_ge(L0["merged"], NG)
                for t in range(1 if last else GB):
                    rows = LAST if last else P
                    where = sums[0:rows, u, 0, t * D:(t + 1) * D]
                    pe.matmul(where, aggT[:, u, t * P:t * P + rows], phm[:, :, :].rearrange("p j b -> p (j b)"),
                              start=True, stop=False, skip_group_check=True)
                    ins = pe.matmul(where, ones_row[0:1, 0:rows], bias_row[0:1, :], start=False, stop=True,
                                    skip_group_check=True)
                ins.then_inc(mid_out, 1)

            sweep(pe, NBAT, 2, [(2, layer_out)])

            def turn_h(b, u, use):
                pe.wait_ge(mid_h, b + 1)
                if later(b, 2):
                    pe.wait_ge(mid_hT, b - 1)
                for t in range(1 if isinstance(b, int) and b == NBAT - 1 else GB):
                    ins = pe.transpose(bank[u][:, t * P:(t + 1) * P], hn[:, u, t, :], ident[:, :])
                ins.then_inc(mid_hT_psum, 1)

            def layer_in(b, u, use):
                pe.wait_ge(mid_hT, b + 1)
                if later(b, 2):
                    pe.wait_ge(mid_wx, b - 1)
                elif isinstance(b, int) and b == 0:
                    pe.wait_ge(self_res, NBAT)
                for t in range(1 if isinstance(b, int) and b == NBAT - 1 else GB):
                    where = sums[:, u, 1, 0:TW] if t == IN_BANK else bank[2 + u][:, t * TW:(t + 1) * TW]
                    ins = pe.matmul(where, hT[:, u, t * P:(t + 1) * P], w1_aug[:, :], start=True, stop=True)
                ins.then_inc(mid_wx_psum, 1)

            sweep(pe, NBAT, 2, [(1, turn_h), (2, layer_in)])
            pe.wait_ge(mid_wx, NBAT)

            def onehotT1(g, s, use):
                pe.wait_ge(L1["onehots"], g + 1)
                if later(g, 1):
                    pe.wait_ge(L1["spread"], g)
                for b in range(GB):
                    ins = pe.transpose(bank[0][:, b * P:(b + 1) * P], onehot[:, s, b, :], ident[:, :])
                ins.then_inc(L1["onehotsT"], 1)

            def targets1(g, s, use):
                pe.wait_ge(L1["spread"], g + 1)
                pe.wait_ge(L1["windowed"][s], 16 * GB * (use + 1))
                if later(g, 1):
                    pe.wait_ge(L1["logits"], 2 * g - 1)
                for b in range(GB):
                    ins = pe.matmul(bank[2][:, b * H:(b + 1) * H], onehotT[:, s % 2, b * P:(b + 1) * P], window[:, s, b, :],
                                    start=True, stop=True)
                ins.then_inc(L1["targets"], 1)

            def turn1(g, s, use):
                pe.wait_ge(L1["logits"], 2 * g + 2)
                if later(g, 1):
                    pe.wait_ge(L1["scanned"], 2 * g - 1)
                for b in range(GB):
                    ins = pe.transpose(bank[1][0:H, b * P:(b + 1) * P], logit[:, s % WGT, b * H:(b + 1) * H], ident[:, :])
                ins.then_inc(L1["msgT"], 1)

            def unturn1(g, s, use):
                pe.wait_ge(L1["dropped"], g + 1)
                if later(g, 1):
                    pe.wait_ge(L1["shifted"], g)
                if later(g, 1):
                    pe.wait_ge(L1["factored"], g)
                pe.matmul(bank[3][:, 64 + s:65 + s], head_spread[:, :], drop[0:H, s:s + 1], start=True, stop=True)
                for b in range(GB):
                    ins = pe.transpose(bank[3][:, b * H:(b + 1) * H], seg_max[0:H, s % 2, b * P:(b + 1) * P], ident[0:H, 0:H])
                ins.then_inc(L1["unturned"], 1)

            def sums1(g, s, use):
                segment_sums(g, s, L1)

            sweep_edges(pe, [(4, turn1), (1, onehotT1), (7, sums1), (2, targets1), (4, unturn1)])

            def turn_out(b, u, use):
                last = isinstance(b, int) and b == NBAT - 1
                pe.wait_ge(fin_num, b + 1)
                pe.wait_ge(fin_den, b + 1)
                if later(b, 2):
                    pe.wait_ge(fin_y, b - 1)
                r = LAST if last else P
                for t in range(1 if last else GB):
                    pe.transpose(bank[u][0:r, t * D:(t + 1) * D], hn_row[:, u, t * P:t * P + r], ident[:, :])
                    ins = pe.matmul(bank[2 + u][0:r, t * H:(t + 1) * H], hT[:, u, t * P:t * P + r], head_pick[:, :],
                                    start=True, stop=True)
                ins.then_inc(fin_psum, 1)

            sweep(pe, NBAT, 2, [(1, turn_out)])


_INS = ["x", "src", "dst", "edge_attr_128", "L0_gnn_phm_rule", "L0_gnn_W", "L0_gnn_bias", "L0_gnn_beta",
        "L1_gnn_W", "L1_gnn_a"]


def kernel(**inputs):
    import numpy as _np
    import concourse.bacc as _bacc
    from concourse.bass_utils import run_bass_kernel_spmd as _run

    nc = _bacc.Bacc("TRN2", target_bir_lowering=False, num_devices=1)
    arrays, args = {}, []
    for name in _INS:
        a = _np.ascontiguousarray(inputs[name])
        if a.ndim == 0:
            a = a.reshape(1)
        arrays[f"in_{name}"] = a
        args.append(nc.dram_tensor(f"in_{name}", a.shape, mybir.dt.from_np(a.dtype), kind="ExternalInput").ap())
    shape = _np.asarray(inputs["x"]).shape
    args.append(nc.dram_tensor("out_0", shape, F32, kind="ExternalOutput").ap())
    gnn_kernel(nc, *args)
    r = _run(nc, [arrays], core_ids=[0])
    return r.results[0]["out_0"]
```
